# Optimizing a Trainium2 kernel written in Bass

```python
import numpy as np
import jax
import jax.numpy as jnp

def _softmax(x, axis=-1):
    return jax.nn.softmax(x, axis=axis)

def _gelu(x):
    return jax.nn.gelu(x, approximate=True)

def _silu(x):
    return jax.nn.silu(x)

def _sigmoid(x):
    return jax.nn.sigmoid(x)

def _layernorm(x, axis=-1, eps=1e-05):
    m = jnp.mean(x, axis=axis, keepdims=True)
    v = jnp.var(x, axis=axis, keepdims=True)
    return (x - m) / jnp.sqrt(v + eps)

def _scatter_add(tgt, idx, src, axis=0):
    return tgt.at[idx].add(src)

def _segment_sum(src, seg, n):
    return jax.ops.segment_sum(src, seg, n)
kernel_name = 'mk_sandwich_d1_jaxref_r8_8caa69'

def setup_inputs(seed: int=0):
    np.random.seed(seed)
    _w = jnp.asarray

    def _L0_attn_setup():
        import jax, jax.numpy as jnp
        from jax import lax
        import numpy as np
        D_MODEL = 128
        D_STATE = 16
        D_CONV = 4
        EXPAND = 2
        D_INNER = EXPAND * D_MODEL
        DT_RANK = D_MODEL // 16
        B, L = (1, 128)

        def _mamba(x, in_w, conv_w, conv_b, xproj_w, dt_w, dt_b, Alog, Dp, out_w):
            xz = x @ in_w.T
            xi, z = jnp.split(xz, 2, axis=-1)
            xc = lax.conv_general_dilated(jnp.swapaxes(xi, 1, 2), conv_w, (1,), [(D_CONV - 1, 0)], feature_group_count=D_INNER)
            u = jnp.swapaxes(jax.nn.silu(xc + conv_b[None, :, None]), 1, 2)
            x_dbl = u @ xproj_w.T
            dt = x_dbl[..., :DT_RANK]
            Bm = x_dbl[..., DT_RANK:DT_RANK + D_STATE]
            Cm = x_dbl[..., DT_RANK + D_STATE:]
            delta = jax.nn.softplus(dt @ dt_w.T + dt_b)
            A = -jnp.exp(Alog)
            dA = jnp.exp(jnp.einsum('bld,dn->bldn', delta, A))
            dBu = jnp.einsum('bld,bln,bld->bldn', delta, Bm, u)

            def step(h, inputs):
                a, b, c = inputs
                h = a * h + b
                return (h, jnp.einsum('bdn,bn->bd', h, c))
            h0 = jnp.zeros((x.shape[0], D_INNER, D_STATE), x.dtype)
            _, ys = lax.scan(step, h0, (jnp.moveaxis(dA, 1, 0), jnp.moveaxis(dBu, 1, 0), jnp.moveaxis(Cm, 1, 0)))
            y = jnp.moveaxis(ys, 0, 1) + u * Dp
            return y * jax.nn.silu(z) @ out_w.T

        def _block(x, fw_in_w, fw_conv_w, fw_conv_b, fw_xproj_w, fw_dt_w, fw_dt_b, fw_Alog, fw_Dp, fw_out_w, bw_in_w, bw_conv_w, bw_conv_b, bw_xproj_w, bw_dt_w, bw_dt_b, bw_Alog, bw_Dp, bw_out_w, proj_w, proj_b, ln_w, ln_b):
            out_fw = _mamba(x, fw_in_w, fw_conv_w, fw_conv_b, fw_xproj_w, fw_dt_w, fw_dt_b, fw_Alog, fw_Dp, fw_out_w) + x
            xb = jnp.flip(x, axis=1)
            out_bw = jnp.flip(_mamba(xb, bw_in_w, bw_conv_w, bw_conv_b, bw_xproj_w, bw_dt_w, bw_dt_b, bw_Alog, bw_Dp, bw_out_w) + xb, axis=1)
            out = jnp.concatenate([out_fw, out_bw], axis=-1) @ proj_w.T + proj_b
            mu = out.mean(-1, keepdims=True)
            var = out.var(-1, keepdims=True)
            return (out - mu) / jnp.sqrt(var + 1e-05) * ln_w + ln_b
        key = jax.random.key(seed)
        ks = jax.random.split(key, 8)

        def nrm(k, shape, s=0.02):
            return jax.random.normal(k, shape, jnp.float32) * s

        def mamba_params(kbase):
            k = jax.random.split(kbase, 7)
            return {'in_w': nrm(k[0], (2 * D_INNER, D_MODEL)), 'conv_w': nrm(k[1], (D_INNER, 1, D_CONV), 0.1), 'conv_b': nrm(k[2], (D_INNER,), 0.1), 'xproj_w': nrm(k[3], (DT_RANK + 2 * D_STATE, D_INNER)), 'dt_w': nrm(k[4], (D_INNER, DT_RANK), 0.1), 'dt_b': nrm(k[5], (D_INNER,), 0.1), 'Alog': jnp.log(jnp.broadcast_to(jnp.arange(1.0, D_STATE + 1, dtype=jnp.float32), (D_INNER, D_STATE))), 'Dp': jnp.ones((D_INNER,), jnp.float32), 'out_w': nrm(k[6], (D_MODEL, D_INNER))}
        fw = mamba_params(ks[0])
        bw = mamba_params(ks[1])
        inp = {'x': jax.random.normal(ks[2], (B, L, D_MODEL), jnp.float32)}
        for n, p in fw.items():
            inp['fw_' + n] = p
        for n, p in bw.items():
            inp['bw_' + n] = p
        inp['proj_w'] = nrm(ks[3], (D_MODEL, 2 * D_MODEL))
        inp['proj_b'] = jnp.zeros((D_MODEL,), jnp.float32)
        inp['ln_w'] = jnp.ones((D_MODEL,), jnp.float32)
        inp['ln_b'] = jnp.zeros((D_MODEL,), jnp.float32)
        return inp
    _L0_attn_in = _L0_attn_setup()

    def _L0_ffn_setup():
        import jax, jax.numpy as jnp
        import numpy as np
        D_IN, D_HID = (128, 512)

        def _ternary(key, shape):
            return jax.random.randint(key, shape, -1, 2).astype(jnp.float32)

        def _tlin(x, w, s):
            return jnp.einsum('bsi,oi->bso', x, w) * s
        key = jax.random.key(seed)
        ks = jax.random.split(key, 12)
        inv = lambda fan: 1.0 / np.sqrt(fan).astype(np.float32)
        return {'x': jax.random.normal(ks[0], (4, 256, D_IN), dtype=jnp.float32), 'w1_w': _ternary(ks[1], (D_HID, D_IN)), 'w1_s': jax.random.uniform(ks[2], (D_HID,), dtype=jnp.float32) * inv(D_IN), 'w2_w': _ternary(ks[3], (D_HID, D_IN)), 'w2_s': jax.random.uniform(ks[4], (D_HID,), dtype=jnp.float32) * inv(D_IN), 'h1_w': _ternary(ks[5], (D_HID, D_HID)), 'h1_s': jax.random.uniform(ks[6], (D_HID,), dtype=jnp.float32) * inv(D_HID), 'h2_w': _ternary(ks[7], (D_HID, D_HID)), 'h2_s': jax.random.uniform(ks[8], (D_HID,), dtype=jnp.float32) * inv(D_HID), 'w3_w': _ternary(ks[9], (D_IN, D_HID)), 'w3_s': jax.random.uniform(ks[10], (D_IN,), dtype=jnp.float32) * inv(D_HID)}
    _L0_ffn_in = _L0_ffn_setup()
    _d = {'L0_attn_x': _L0_attn_in['x'], 'L0_attn_fw_in_w': _L0_attn_in['fw_in_w'], 'L0_attn_fw_conv_w': _L0_attn_in['fw_conv_w'], 'L0_attn_fw_conv_b': _L0_attn_in['fw_conv_b'], 'L0_attn_fw_xproj_w': _L0_attn_in['fw_xproj_w'], 'L0_attn_fw_dt_w': _L0_attn_in['fw_dt_w'], 'L0_attn_fw_dt_b': _L0_attn_in['fw_dt_b'], 'L0_attn_fw_Alog': _L0_attn_in['fw_Alog'], 'L0_attn_fw_Dp': _L0_attn_in['fw_Dp'], 'L0_attn_fw_out_w': _L0_attn_in['fw_out_w'], 'L0_attn_bw_in_w': _L0_attn_in['bw_in_w'], 'L0_attn_bw_conv_w': _L0_attn_in['bw_conv_w'], 'L0_attn_bw_conv_b': _L0_attn_in['bw_conv_b'], 'L0_attn_bw_xproj_w': _L0_attn_in['bw_xproj_w'], 'L0_attn_bw_dt_w': _L0_attn_in['bw_dt_w'], 'L0_attn_bw_dt_b': _L0_attn_in['bw_dt_b'], 'L0_attn_bw_Alog': _L0_attn_in['bw_Alog'], 'L0_attn_bw_Dp': _L0_attn_in['bw_Dp'], 'L0_attn_bw_out_w': _L0_attn_in['bw_out_w'], 'L0_attn_proj_w': _L0_attn_in['proj_w'], 'L0_attn_proj_b': _L0_attn_in['proj_b'], 'L0_attn_ln_w': _L0_attn_in['ln_w'], 'L0_attn_ln_b': _L0_attn_in['ln_b'], 'L0_ffn_w1_w': _L0_ffn_in['w1_w'], 'L0_ffn_w1_s': _L0_ffn_in['w1_s'], 'L0_ffn_w2_w': _L0_ffn_in['w2_w'], 'L0_ffn_w2_s': _L0_ffn_in['w2_s'], 'L0_ffn_h1_w': _L0_ffn_in['h1_w'], 'L0_ffn_h1_s': _L0_ffn_in['h1_s'], 'L0_ffn_h2_w': _L0_ffn_in['h2_w'], 'L0_ffn_h2_s': _L0_ffn_in['h2_s'], 'L0_ffn_w3_w': _L0_ffn_in['w3_w'], 'L0_ffn_w3_s': _L0_ffn_in['w3_s']}
    _x0 = _d['L0_attn_x']
    _d['L0_attn_x'] = jax.random.normal(jax.random.fold_in(jax.random.key(seed), 1), (16, 256, 128), dtype=_x0.dtype)
    del _x0
    return _d

def reference(L0_attn_x, L0_attn_fw_in_w, L0_attn_fw_conv_w, L0_attn_fw_conv_b, L0_attn_fw_xproj_w, L0_attn_fw_dt_w, L0_attn_fw_dt_b, L0_attn_fw_Alog, L0_attn_fw_Dp, L0_attn_fw_out_w, L0_attn_bw_in_w, L0_attn_bw_conv_w, L0_attn_bw_conv_b, L0_attn_bw_xproj_w, L0_attn_bw_dt_w, L0_attn_bw_dt_b, L0_attn_bw_Alog, L0_attn_bw_Dp, L0_attn_bw_out_w, L0_attn_proj_w, L0_attn_proj_b, L0_attn_ln_w, L0_attn_ln_b, L0_ffn_w1_w, L0_ffn_w1_s, L0_ffn_w2_w, L0_ffn_w2_s, L0_ffn_h1_w, L0_ffn_h1_s, L0_ffn_h2_w, L0_ffn_h2_s, L0_ffn_w3_w, L0_ffn_w3_s):

    def _L0_attn_ref(x, fw_in_w, fw_conv_w, fw_conv_b, fw_xproj_w, fw_dt_w, fw_dt_b, fw_Alog, fw_Dp, fw_out_w, bw_in_w, bw_conv_w, bw_conv_b, bw_xproj_w, bw_dt_w, bw_dt_b, bw_Alog, bw_Dp, bw_out_w, proj_w, proj_b, ln_w, ln_b):
        import jax, jax.numpy as jnp
        from jax import lax
        import numpy as np
        D_MODEL = 128
        D_STATE = 16
        D_CONV = 4
        EXPAND = 2
        D_INNER = EXPAND * D_MODEL
        DT_RANK = D_MODEL // 16
        B, L = (1, 128)

        def _mamba(x, in_w, conv_w, conv_b, xproj_w, dt_w, dt_b, Alog, Dp, out_w):
            xz = x @ in_w.T
            xi, z = jnp.split(xz, 2, axis=-1)
            xc = lax.conv_general_dilated(jnp.swapaxes(xi, 1, 2), conv_w, (1,), [(D_CONV - 1, 0)], feature_group_count=D_INNER)
            u = jnp.swapaxes(jax.nn.silu(xc + conv_b[None, :, None]), 1, 2)
            x_dbl = u @ xproj_w.T
            dt = x_dbl[..., :DT_RANK]
            Bm = x_dbl[..., DT_RANK:DT_RANK + D_STATE]
            Cm = x_dbl[..., DT_RANK + D_STATE:]
            delta = jax.nn.softplus(dt @ dt_w.T + dt_b)
            A = -jnp.exp(Alog)
            dA = jnp.exp(jnp.einsum('bld,dn->bldn', delta, A))
            dBu = jnp.einsum('bld,bln,bld->bldn', delta, Bm, u)

            def step(h, inputs):
                a, b, c = inputs
                h = a * h + b
                return (h, jnp.einsum('bdn,bn->bd', h, c))
            h0 = jnp.zeros((x.shape[0], D_INNER, D_STATE), x.dtype)
            _, ys = lax.scan(step, h0, (jnp.moveaxis(dA, 1, 0), jnp.moveaxis(dBu, 1, 0), jnp.moveaxis(Cm, 1, 0)))
            y = jnp.moveaxis(ys, 0, 1) + u * Dp
            return y * jax.nn.silu(z) @ out_w.T

        def _block(x, fw_in_w, fw_conv_w, fw_conv_b, fw_xproj_w, fw_dt_w, fw_dt_b, fw_Alog, fw_Dp, fw_out_w, bw_in_w, bw_conv_w, bw_conv_b, bw_xproj_w, bw_dt_w, bw_dt_b, bw_Alog, bw_Dp, bw_out_w, proj_w, proj_b, ln_w, ln_b):
            out_fw = _mamba(x, fw_in_w, fw_conv_w, fw_conv_b, fw_xproj_w, fw_dt_w, fw_dt_b, fw_Alog, fw_Dp, fw_out_w) + x
            xb = jnp.flip(x, axis=1)
            out_bw = jnp.flip(_mamba(xb, bw_in_w, bw_conv_w, bw_conv_b, bw_xproj_w, bw_dt_w, bw_dt_b, bw_Alog, bw_Dp, bw_out_w) + xb, axis=1)
            out = jnp.concatenate([out_fw, out_bw], axis=-1) @ proj_w.T + proj_b
            mu = out.mean(-1, keepdims=True)
            var = out.var(-1, keepdims=True)
            return (out - mu) / jnp.sqrt(var + 1e-05) * ln_w + ln_b
        return _block(x, fw_in_w, fw_conv_w, fw_conv_b, fw_xproj_w, fw_dt_w, fw_dt_b, fw_Alog, fw_Dp, fw_out_w, bw_in_w, bw_conv_w, bw_conv_b, bw_xproj_w, bw_dt_w, bw_dt_b, bw_Alog, bw_Dp, bw_out_w, proj_w, proj_b, ln_w, ln_b)

    def _L0_ffn_ref(x, w1_w, w1_s, w2_w, w2_s, h1_w, h1_s, h2_w, h2_s, w3_w, w3_s):
        import jax, jax.numpy as jnp
        import numpy as np
        D_IN, D_HID = (128, 512)

        def _ternary(key, shape):
            return jax.random.randint(key, shape, -1, 2).astype(jnp.float32)

        def _tlin(x, w, s):
            return jnp.einsum('bsi,oi->bso', x, w) * s
        h = jax.nn.silu(_tlin(x, w1_w, w1_s)) * _tlin(x, w2_w, w2_s)
        h = jax.nn.gelu(_tlin(h, h1_w, h1_s), approximate=False)
        h = jax.nn.gelu(_tlin(h, h2_w, h2_s), approximate=False)
        return _tlin(h, w3_w, w3_s)
    x = L0_attn_x
    x = x + _layernorm(_L0_attn_ref(_layernorm(x, axis=-1), L0_attn_fw_in_w, L0_attn_fw_conv_w, L0_attn_fw_conv_b, L0_attn_fw_xproj_w, L0_attn_fw_dt_w, L0_attn_fw_dt_b, L0_attn_fw_Alog, L0_attn_fw_Dp, L0_attn_fw_out_w, L0_attn_bw_in_w, L0_attn_bw_conv_w, L0_attn_bw_conv_b, L0_attn_bw_xproj_w, L0_attn_bw_dt_w, L0_attn_bw_dt_b, L0_attn_bw_Alog, L0_attn_bw_Dp, L0_attn_bw_out_w, L0_attn_proj_w, L0_attn_proj_b, L0_attn_ln_w, L0_attn_ln_b), axis=-1)
    x = x + _layernorm(_L0_ffn_ref(_layernorm(x, axis=-1), L0_ffn_w1_w, L0_ffn_w1_s, L0_ffn_w2_w, L0_ffn_w2_s, L0_ffn_h1_w, L0_ffn_h1_s, L0_ffn_h2_w, L0_ffn_h2_s, L0_ffn_w3_w, L0_ffn_w3_s), axis=-1)
    return x

_drawn_inputs = setup_inputs


def setup_inputs(seed=0):
    import zlib

    import numpy as np

    out = dict(_drawn_inputs(seed))
    spreads = {'L0_attn_fw_Dp': (1.0, 0.6),
     'L0_attn_bw_Dp': (1.0, 0.6),
     'L0_attn_proj_b': (0.0, 0.1),
     'L0_attn_ln_w': (1.0, 0.2),
     'L0_attn_ln_b': (0.0, 0.1)}
    factors = {'L0_attn_fw_in_w': 8.0,
     'L0_attn_fw_conv_w': 8.0,
     'L0_attn_fw_conv_b': 8.0,
     'L0_attn_fw_xproj_w': 8.0,
     'L0_attn_fw_dt_w': 8.0,
     'L0_attn_fw_dt_b': 8.0,
     'L0_attn_fw_Alog': 8.0,
     'L0_attn_fw_out_w': 8.0,
     'L0_attn_bw_in_w': 8.0,
     'L0_attn_bw_conv_w': 8.0,
     'L0_attn_bw_conv_b': 8.0,
     'L0_attn_bw_xproj_w': 8.0,
     'L0_attn_bw_dt_w': 8.0,
     'L0_attn_bw_dt_b': 8.0,
     'L0_attn_bw_Alog': 8.0,
     'L0_attn_bw_out_w': 8.0}
    for name, (base, spread) in spreads.items():
        noise = np.random.default_rng([zlib.crc32(name.encode()), seed]).standard_normal(out[name].shape)
        drawn = base * np.exp(spread * noise) if base else spread * noise
        out[name] = jnp.asarray(drawn.astype(out[name].dtype))
    for name, factor in factors.items():
        out[name] = (out[name] * factor).astype(out[name].dtype)
    return out
```

```python
import concourse.bass as bass
from concourse import mybir
from contextlib import ExitStack

SEQS, L, C = 16, 256, 128
DI, NS, RANK, TAPS = 256, 16, 8, 4
HID = 512
SPG = 2
T = SPG * L
G = SEQS // SPG
NT = T // 128
DT = DI // 128
NQ = 2 * DT
NJ, DW = 4, 32
NK = NS // NJ
NR = 128 // DW
UNITS = NQ * NK * NR
UQ = NK * NR
PAD = TAPS - 1
LP = L + 2 * PAD
HT = HID // 128
EPS = 1e-5
SMALL = 2.0 ** -7
NDB = 4

PE_FRONT = ["xT"] + [f"conv{q}" for q in range(NQ)] + ["xd0", "xd1"] \
    + [f"dt{q}" for q in range(NQ)] + [f"z{q}" for q in range(NQ)]
ACT_FRONT = ["xT"] + [f"conv{q}" for q in range(NQ)] + ["silu_u", "xd0", "xd1"] \
    + [f"dt{q}" for q in range(NQ)] + ["abs", "exp", "square"] + [f"z{q}" for q in range(NQ)] + ["silu_z", "ln"]
DVE_FRONT = ["stats", "aggr", "var", "norm", "series", "large", "select", "delta", "du"]
PE_BACK = ["combine", "xT"] + [f"a{m}" for m in range(HT)] + [f"b{m}" for m in range(HT)] \
    + [f"h1_{m}" for m in range(HT)] + [f"h2_{m}" for m in range(HT)] + ["w3"]
ACT_BACK = ["xT"] + [f"a{m}" for m in range(HT)] + ["silu"] + [f"h1_{m}" for m in range(HT)] + ["gelu1"] \
    + [f"h2_{m}" for m in range(HT)] + ["gelu2"]
DVE_BACK = ["stats_a", "aggr_a", "var_a", "norm_a", "lnw", "lnb", "stats_b", "aggr_b", "var_b", "norm_b",
            "res_b", "stats_c", "aggr_c", "var_c", "norm_c"] + [f"b{m}" for m in range(HT)] \
    + ["stats_d", "aggr_d", "var_d", "norm_d", "res_d"]
POOL_BACK = ["rstd_a", "rstd_b", "rstd_c", "rstd_d"]


def build(nc, x, fw, bw, proj_w, proj_b, ln_w, ln_b, w1, s1, w2, s2, h1, h1s, h2, h2s, w3, w3s, out):
    f32 = mybir.dt.float32
    ALU, ACT, AX = mybir.AluOpType, mybir.ActivationFunctionType, mybir.AxisListType
    MAMBA = (fw, bw)

    dd = nc.dram_tensor("delta_and_du", (2, NQ, 2, 128, T), f32).ap()
    bc = nc.dram_tensor("b_and_c", (2, 2, 2 * NS, T), f32).ap()
    x_g = x.rearrange("(g s) (h p) c -> g p (s h) c", s=SPG, p=128)
    out_g = out.rearrange("(g s) (h p) c -> g p (s h) c", s=SPG, p=128)

    with ExitStack() as ctx:
        def sb(name, shape):
            return ctx.enter_context(nc.sbuf_tensor(name, shape, f32))

        def pb(name, shape=(128, T)):
            return ctx.enter_context(nc.psum_tensor(name, list(shape), f32))

        def sem(name):
            return ctx.enter_context(nc.semaphore(name))

        REP = sb("rep", [128, 2, 2 * NR, T])
        BC = sb("bc_rep", [128, 2, 2 * NK, T])
        DB = sb("dbu", [128, NDB, T])
        PR = sb("prod", [128, 2, NR, T])
        AR = sb("a_rep", [128, 2 * 8, NK])
        XT = sb("x_tok", [128, NT, C])
        XNT = sb("xn_t", [128, 2, SPG, LP])
        U = sb("u", [128, 2, NQ, T])
        SZ = sb("silu_z", [128, 2, NQ, T])
        SPA = sb("dt_raw", [128, NQ, T])
        SPB = sb("delta", [128, NQ, T])
        TA = sb("normed", [128, NT, C])
        X1 = sb("x1", [128, NT, C])
        X2T = sb("x2_t", [128, T])
        XRES = X2T[:, :].rearrange("p (t c) -> p t c", c=C)
        FA = sb("ffn_a", [128, HT, T])
        FG = sb("ffn_g", [128, HT, T])
        XD = FG[0:RANK + 2 * NS, 0:2, :]
        STF, MVF, RSF = sb("stf", [128, NT, 6]), sb("mvf", [128, NT, 2]), sb("rsf", [128, 2, NT])
        STB, MVB, RSB = sb("stb", [128, NT, 6]), sb("mvb", [128, NT, 2]), sb("rsb", [128, 2, NT])
        ident = sb("ident", [128, 128])
        fold = sb("fold", [128, DW])
        mhalf = sb("minus_half", [128, NT])
        zero2 = sb("zero2", [128, SPG])
        ones = sb("ones", [1, 128])
        pbrow = sb("proj_b_row", [1, C])
        lnw, lnb = sb("lnw", [128, C]), sb("lnb", [128, C])
        tapT = sb("tap_t", [128, 2, TAPS, DI])
        zT = sb("z_t", [128, NQ, 128])
        xpT = sb("xproj_t", [128, NQ, RANK + 2 * NS])
        dtT = sb("dt_t", [RANK, NQ, 128])
        P12 = sb("proj_sum_t", [128, 128])
        WE = sb("w_eff", [128, NQ, C])
        DD = sb("d_diag", [128, NQ, 128])
        w1T, w2T = sb("w1_t", [128, HID]), sb("w2_t", [128, HID])
        h1T, h2T = sb("h1_t", [128, HT, HID]), sb("h2_t", [128, HT, HID])
        w3T = sb("w3_t", [128, HT, C])
        cw = sb("conv_w_cols", [128, NQ, TAPS])
        cb, db, dp = sb("conv_b_cols", [128, NQ]), sb("dt_b_cols", [128, NQ]), sb("d_cols", [128, NQ])
        s1c, s2c, h1c, h2c = (sb(n, [128, HT]) for n in ("s1c", "s2c", "h1c", "h2c"))
        w3c = sb("w3c", [128, 1])
        root = sb("minus_root", [128, 1])
        big = TA[:, :, :].rearrange("p t c -> p (t c)").bitcast(mybir.dt.uint8) \
            .rearrange("p (q l) -> p q l", q=NQ)
        PT = PR[:, 0, 0, 0:2 * 128].rearrange("p (d c) -> p d c", d=2)
        n_in = REP[:, 0, 0:2, :].rearrange("p a (b c) -> p (a b) c", c=128)
        n_tap = REP[:, 0, 2:6, :].rearrange("p a (b c) -> p (a b) c", c=128)
        n_xp = REP[0:RANK + 2 * NS, 0, 6, :].rearrange("p (q c) -> p q c", c=128)
        n_dt = REP[:, 0, 7, 0:NQ * RANK].rearrange("p (q r) -> p q r", r=RANK)
        n_out = REP[:, 1, 0, :].rearrange("p (q c) -> p q c", c=128)
        n_proj = REP[:, 1, 1, 0:2 * C].rearrange("p (q c) -> p q c", c=128)
        n_w3 = REP[:, 1, 2, :].rearrange("p (q c) -> p q c", c=128)
        n_w3s = REP[:, 1, 3, :].rearrange("p (q c) -> p q c", c=128)
        n_w1 = REP[:, 1, 4, :].rearrange("p (q c) -> p q c", c=128)
        n_w2 = REP[:, 1, 5, :].rearrange("p (q c) -> p q c", c=128)
        n_al = REP[:, 1, 6, 0:2 * 8 * NS].rearrange("p (a n) -> p a n", n=NS)
        n_ex = REP[:, 1, 7, 0:2 * 8 * NK].rearrange("p (a n) -> p a n", n=NK)
        n_h1 = BC[:, 0, 0:HT, :]
        n_h2 = BC[:, 0, HT:2 * HT, :]

        dA = [pb(f"dA{i}", (128, SPG, L)) for i in range(2)]
        HP = [pb(f"h{i}") for i in range(2)]
        Y = pb("y")
        GF = pb("front_bank")
        GB = [pb(f"back_bank{i}") for i in range(2)]

        w_in = sem("w_in")
        w_in2 = sem("w_in2")
        const_ok = sem("const_ok")
        dprep = sem("dprep")
        w_pe = sem("w_pe")
        w_act, w_dve = sem("w_act"), sem("w_dve")
        a_exp = sem("a_exp")
        dA_ready, dbu_ready = sem("dA_ready"), sem("dbu_ready")
        scan_done, prod_ready = sem("scan_done"), sem("prod_ready")
        zero_set = sem("zero_set")
        sums_done = sem("sums_done")
        y_ready, gated = sem("y_ready"), sem("gated")
        rep_in = [sem("rep_in0"), sem("rep_in1")]
        bc_in = [sem("bc_in0"), sem("bc_in1")]
        x_in, xres_in, out_done = sem("x_in"), sem("xres_in"), sem("out_done")
        bc_out, dd_out = sem("bc_out"), sem("dd_out")
        pe_front, act_front, dve_front, pool_front = (sem(n) for n in ("pe_front", "act_front", "dve_front", "pool_front"))
        pe_back, act_back, dve_back, pool_back = (sem(n) for n in ("pe_back", "act_back", "dve_back", "pool_back"))

        TABLES = {"pe_front": (pe_front, PE_FRONT), "act_front": (act_front, ACT_FRONT),
                  "dve_front": (dve_front, DVE_FRONT), "pool_front": (pool_front, ["rstd"]),
                  "pe_back": (pe_back, PE_BACK), "act_back": (act_back, ACT_BACK),
                  "dve_back": (dve_back, DVE_BACK), "pool_back": (pool_back, POOL_BACK)}

        def wait(eng, s, value):
            if not isinstance(value, int) or value > 0:
                eng.wait_ge(s, value)

        def after(eng, table, step, g):
            s, steps = TABLES[table]
            if isinstance(g, int) and g < 0:
                return
            wait(eng, s, g * len(steps) + steps.index(step) + 1)

        def unit(p):
            q = p // UQ
            return q // DT, q % DT, (p % UQ) // NR, p % NR

        batches = [([n_tap[:, (d * DT + t) * TAPS + k, :] for k in range(TAPS)], tapT[:, d, :, 128 * t:128 * (t + 1)])
                   for d in range(2) for t in range(DT)]
        batches.append(([n_in[:, 4 * d + DT + t, :] for d in range(2) for t in range(DT)], zT[:, :, :]))
        batches.append(([n_xp[:, q, :] for q in range(NQ)], xpT[:, :, :]))
        batches.append(([n_dt[:, q, :] for q in range(NQ)], dtT[:, :, :]))
        N_PT = len(batches)
        batches.append(([n_proj[:, d, :] for d in range(2)], PT[:, :, :]))
        batches += [([n[:, m, :] for m in range(HT)], w[:, :].rearrange("p (m c) -> p m c", c=128))
                    for n, w in ((n_w1, w1T), (n_w2, w2T))]
        batches.append(([n_w3s[:, m, :] for m in range(HT)], w3T[:, :, :]))
        N_H = len(batches)
        batches += [([n[:, m, 128 * k:128 * (k + 1)] for m in range(HT)],
                     w[:, k, :].rearrange("p (m c) -> p m c", c=128))
                    for n, w in ((n_h1, h1T), (n_h2, h2T)) for k in range(HT)]
        N_WE = len(batches)
        copies = [dst for _, dst in batches] + [WE[:, :, :]]
        NB_W = len(copies)
        W_DMAS = 2 * (5 + 3 + NJ) + 2 + 2 + 4 + 1 + 2 + 1
        DVE_SETUP = ["scaled", "fold", "d_diag", "a_rep", "p12"]

        def in_bank(n):
            p, a, c = copies[n].shape
            return GB[n % 2][0:p, 0:a * c].rearrange("p (a c) -> p a c", c=c)

        block = ctx.enter_context(nc.Block())

        @block.sync
        def _(sp):
            def rep_load(q, g, par, slot):
                for j in range(NJ):
                    sp.dma_start(REP[DW * j:DW * (j + 1), slot, :, :],
                                 dd[par, q].rearrange("t (r p) l -> p (t r) l", p=DW)).then_inc(rep_in[slot], 16)

            def bc_load(d, g, par):
                for j in range(NJ):
                    rows = bc[par, d].rearrange("(m j) l -> j m l", j=NJ)[j:j + 1]
                    sp.dma_start(BC[DW * j:DW * (j + 1), d, :, :],
                                 rows.to_broadcast([DW, 2 * NK, T])).then_inc(bc_in[d], 16)

            def half_free(q, g):
                wait(sp, dA_ready, g * UNITS + UQ * (q + 1))
                wait(sp, dbu_ready, g * UNITS + UQ * (q + 1))

            def bc_free(d, g):
                wait(sp, dbu_ready, g * UNITS + 2 * UQ * (d + 1))
                wait(sp, prod_ready, g * UNITS + 2 * UQ * (d + 1))

            def bc_store(f, par):
                if not (isinstance(f, int) and f < 2):
                    wait(sp, bc_in[0], (f - 1) * 64)
                    wait(sp, bc_in[1], (f - 1) * 64)
                for d in range(2):
                    after(sp, "act_front", f"xd{d}", f)
                    sp.dma_start(bc[par, d], XD[RANK:RANK + 2 * NS, d, :]).then_inc(bc_out, 16)

            def dd_store(f, par):
                if not (isinstance(f, int) and f < 2):
                    wait(sp, rep_in[0], (f - 1) * 128)
                    wait(sp, rep_in[1], (f - 1) * 128)
                after(sp, "dve_front", "delta", f)
                sp.dma_start(dd[par, :, 0].rearrange("q p l -> p q l"), SPB[:, :, :]).then_inc(dd_out, 16)
                after(sp, "dve_front", "du", f)
                sp.dma_start(dd[par, :, 1].rearrange("q p l -> p q l"), SPA[:, :, :]).then_inc(dd_out, 16)

            def iteration(g, par, front, back):
                f, b = g + 1, g - 1
                fp = 1 - par
                if front:
                    after(sp, "pe_front", "xT", f - 1)
                    sp.dma_start(XT[:, :, :], x_g[f]).then_inc(x_in, 16)
                if back:
                    sp.dma_start(XRES, x_g[b]).then_inc(xres_in, 16)
                half_free(3, g - 1)
                rep_load(1, g, par, 1)
                bc_free(1, g - 1)
                bc_load(1, g, par)
                half_free(0, g)
                rep_load(2, g, par, 0)
                if front:
                    bc_store(f, fp)
                half_free(1, g)
                rep_load(3, g, par, 1)
                if front:
                    bc_free(0, g)
                    wait(sp, bc_out, (f + 1) * 32)
                    bc_load(0, f, fp)
                    dd_store(f, fp)
                    half_free(2, g)
                    wait(sp, dd_out, (f + 1) * 32)
                    rep_load(0, f, fp, 0)
                if back:
                    after(sp, "dve_back", "res_d", b)
                    sp.dma_start(out_g[b], X1[:, :, :]).then_inc(out_done, 16)

            sp.dma_start(XT[:, :, :], x_g[0]).then_inc(x_in, 16)
            for d, m in enumerate(MAMBA):
                sp.dma_start(n_in[:, 4 * d:4 * d + 4, :], m["in_w"].rearrange("(t p) c -> p t c", p=128)).then_inc(w_in, 16)
                sp.dma_start(cw[:, DT * d:DT * d + DT, :], m["conv_w"].rearrange("(t p) a k -> p t (a k)", p=128)).then_inc(w_in, 16)
                sp.dma_start(n_xp[:, DT * d:DT * d + DT, :], m["xproj_w"].rearrange("o (t c) -> o t c", c=128)).then_inc(w_in, 16)
                sp.dma_start(n_dt[:, DT * d:DT * d + DT, :], m["dt_w"].rearrange("(t p) r -> p t r", p=128)).then_inc(w_in, 16)
                sp.dma_start(n_out[:, DT * d:DT * d + DT, :], m["out_w"].rearrange("o (t c) -> o t c", c=128)).then_inc(w_in, 16)
                for cols, name in ((cb, "conv_b"), (db, "dt_b"), (dp, "Dp")):
                    sp.dma_start(cols[:, DT * d:DT * d + DT], m[name].rearrange("(t p) -> p t", p=128),
                                 allow_slow_non_contiguous=True).then_inc(w_in, 16)
                for j in range(NJ):
                    sp.dma_start(n_al[DW * j:DW * (j + 1), 8 * d:8 * d + 8, :],
                                 m["Alog"].rearrange("(a p) n -> p a n", p=DW)).then_inc(w_in, 16)
            sp.dma_start(n_proj, proj_w.rearrange("o (t c) -> o t c", c=128)).then_inc(w_in, 16)
            sp.dma_start(pbrow[:, :], proj_b.rearrange("(a c) -> a c", a=1)).then_inc(w_in, 16)
            for t_, v in ((lnw, ln_w), (lnb, ln_b)):
                sp.dma_start(t_[:, :], v.rearrange("(a c) -> a c", a=1).to_broadcast([128, C])).then_inc(w_in, 16)
            for cols, v in ((s1c, s1), (s2c, s2), (h1c, h1s), (h2c, h2s)):
                sp.dma_start(cols[:, :], v.rearrange("(t p) -> p t", p=128),
                             allow_slow_non_contiguous=True).then_inc(w_in, 16)
            sp.dma_start(w3c[:, :], w3s.rearrange("(p a) -> p a", a=1)).then_inc(w_in, 16)
            for t_, w in ((n_w1, w1), (n_w2, w2)):
                sp.dma_start(t_, w.rearrange("(t p) c -> p t c", p=128)).then_inc(w_in, 16)
            sp.dma_start(n_w3, w3.rearrange("o (t c) -> o t c", c=128)).then_inc(w_in, 16)
            for t_, w in ((n_h1, h1), (n_h2, h2)):
                sp.dma_start(t_, w.rearrange("(t p) c -> p t c", p=128)).then_inc(w_in2, 16)

            sp.sem_inc(out_done, 16)
            bc_store(0, 0)
            wait(sp, bc_out, 32)
            sp.wait_ge(w_pe, NB_W)
            sp.wait_ge(dprep, len(DVE_SETUP))
            bc_load(0, 0, 0)
            dd_store(0, 0)
            wait(sp, dd_out, 32)
            rep_load(0, 0, 0, 0)

            iteration(0, 0, True, False)
            with sp.Fori(0, G // 2 - 1) as i:
                iteration(2 * i + 1, 1, True, True)
                iteration(2 * i + 2, 0, True, True)
            iteration(G - 1, 1, False, True)
            sp.dma_start(XRES, x_g[G - 1]).then_inc(xres_in, 16)
            after(sp, "dve_back", "res_d", G - 1)
            sp.dma_start(out_g[G - 1], X1[:, :, :]).then_inc(out_done, 16)
            sp.wait_ge(out_done, 16 * (G + 1))

        @block.gpsimd
        def _(pool):
            def rstd_front(f):
                after(pool, "dve_front", "var", f)
                nc.gpsimd.tensor_tensor(RSF[:, 1, :], RSF[:, 0, :], mhalf[:, :], ALU.pow).then_inc(pool_front, 1)

            def rstd_back(n, b):
                after(pool, "dve_back", "var_" + n, b)
                nc.gpsimd.tensor_tensor(RSB[:, 1, :], RSB[:, 0, :], mhalf[:, :], ALU.pow).then_inc(pool_back, 1)

            def iteration(g, par, front, back):
                f, b = g + 1, g - 1
                for p in range(UNITS):
                    d, dt, k, r = unit(p)
                    slot = (p // UQ) % 2
                    if p % UQ == 0:
                        pool.wait_ge(rep_in[slot], 64 * (2 * g + p // UQ // 2 + 1))
                    if p % (2 * UQ) == 0:
                        pool.wait_ge(bc_in[d], 64 * (g + 1))
                    wait(pool, scan_done, g * UNITS + p - NDB + 1)
                    nc.gpsimd.tensor_tensor(DB[:, p % NDB, :], REP[:, slot, NR + r, :], BC[:, d, k, :],
                                            ALU.mult).then_inc(dbu_ready, 1)
                    if front and p == 4:
                        rstd_front(f)
                    if back:
                        for n, at in (("a", 10), ("b", 14), ("c", 18), ("d", 61)):
                            if p == at:
                                rstd_back(n, b)

            nc.gpsimd.memset(ident[:, :], 0.0).then_inc(const_ok, 1)
            nc.gpsimd.memset(mhalf[:, :], -0.5)
            nc.gpsimd.memset(zero2[:, :], 0.0)
            nc.gpsimd.memset(root[:, :], -(3.0 ** 0.5) / 4)
            nc.gpsimd.memset(ones[:, :], 1.0)
            nc.gpsimd.memset(XNT[:, :, :, :], 0.0)
            pool.wait_ge(const_ok, 1)
            nc.gpsimd.affine_select(out=ident[:, :], in_=ident[:, :], compare_op=ALU.not_equal, fill=1.0,
                                    base=0, pattern=[[-1, 128]], channel_multiplier=1).then_inc(const_ok, 1)
            pool.wait_ge(const_ok, 2)
            rstd_front(0)
            iteration(0, 0, True, False)
            with pool.Fori(0, G // 2 - 1) as i:
                iteration(2 * i + 1, 1, True, True)
                iteration(2 * i + 2, 0, True, True)
            iteration(G - 1, 1, False, True)
            for n in "abcd":
                rstd_back(n, G - 1)

        @block.scalar
        def _(act):
            act_fn = nc.scalar.activation

            def front_xT(f, par):
                after(act, "pe_front", "xT", f)
                after(act, "pe_back", "combine", f - 2)
                act_fn(XNT[:, par, :, PAD:PAD + L], GF[:, :].rearrange("p (s l) -> p s l", s=SPG),
                       ACT.Copy).then_inc(act_front, 1)

            def front_conv(q, f, par):
                after(act, "pe_front", f"conv{q}", f)
                act_fn(U[:, par, q, :], GF[:, :], ACT.Identity, bias=cb[:, q:q + 1]).then_inc(act_front, 1)

            def front_z(q, f, par):
                after(act, "pe_front", f"z{q}", f)
                act_fn(SZ[:, par, q, :], GF[:, :], ACT.Copy).then_inc(act_front, 1)

            def silu_u(f, par):
                after(act, "act_front", f"conv{NQ - 1}", f)
                act_fn(U[:, par], U[:, par], ACT.Silu).then_inc(act_front, 1)

            def silus(f, par, b, front, back):
                if front:
                    after(act, "act_front", f"z{NQ - 1}", f)
                    act_fn(SZ[:, par], SZ[:, par], ACT.Silu).then_inc(act_front, 1)
                if back:
                    after(act, "act_back", f"a{HT - 1}", b)
                    act_fn(FA[:, :, :], FA[:, :, :], ACT.Silu).then_inc(act_back, 1)

            def front_xd(d, f):
                after(act, "pe_front", f"xd{d}", f)
                if not (isinstance(f, int) and f < 1):
                    wait(act, bc_out, f * 32)
                act_fn(XD[:, d, :], GF[0:RANK + 2 * NS, :], ACT.Copy).then_inc(act_front, 1)

            def front_dt(q, f):
                after(act, "pe_front", f"dt{q}", f)
                if not (isinstance(f, int) and f < 1):
                    wait(act, dd_out, f * 32)
                act_fn(SPA[:, q, :], GF[:, :], ACT.Identity, bias=db[:, q:q + 1]).then_inc(act_front, 1)

            def front_soft(f):
                after(act, "act_front", f"dt{NQ - 1}", f)
                act_fn(SPB[:, :, :], SPA[:, :, :], ACT.Abs).then_inc(act_front, 1)
                after(act, "act_front", "abs", f)
                act_fn(SPB[:, :, :], SPB[:, :, :], ACT.Exp, scale=-1.0).then_inc(act_front, 1)
                after(act, "act_front", "exp", f)
                act.wait_ge(bc_out, 32 * (f + 1))
                act_fn(FG[:, :, :], SPB[:, :, :], ACT.Square, scale=3.0 ** -0.5,
                       bias=root[:, 0:1]).then_inc(act_front, 1)

            def front_ln(f):
                after(act, "dve_front", "large", f)
                act_fn(SPB[:, :, :], SPB[:, :, :], ACT.Ln, bias=1.0).then_inc(act_front, 1)

            def back_xT(b):
                after(act, "pe_back", "xT", b)
                act_fn(X2T[:, :], GB[1][:, :], ACT.Copy).then_inc(act_back, 1)

            def back_a(m, b):
                after(act, "pe_back", f"a{m}", b)
                act_fn(FA[:, m, :], GB[m % 2][:, :], ACT.Copy, scale=s1c[:, m:m + 1]).then_inc(act_back, 1)

            def back_h(n, m, b):
                dst, col = ((FG, h1c), (FA, h2c))[n - 1]
                if n == 1 and m == 0 and not (isinstance(b, int) and b > G - 3):
                    after(act, "dve_front", "delta", b + 2)
                after(act, "pe_back", f"h{n}_{m}", b)
                act_fn(dst[:, m, :], GB[m % 2][:, :], ACT.Copy, scale=col[:, m:m + 1]).then_inc(act_back, 1)

            def gelu(n, b):
                buf = (FG, FA)[n - 1]
                after(act, "act_back", f"h{n}_{HT - 1}", b)
                act_fn(buf[:, :, :], buf[:, :, :], ACT.Gelu).then_inc(act_back, 1)

            def iteration(g, par, front, back):
                f, b, fp = g + 1, g - 1, 1 - par
                for p in range(UNITS):
                    d, dt, k, r = unit(p)
                    slot = (p // UQ) % 2
                    first = 0 if d == 0 else L - 1
                    lo, hi = (1, L) if d == 0 else (0, L - 1)
                    wait(act, scan_done, g * UNITS + p - 1)
                    if p % (2 * UQ) < 2:
                        act_fn(dA[p % 2][:, :, first], zero2[:, :], ACT.Copy).then_inc(zero_set, 1)
                    if p % UQ == 0:
                        act.wait_ge(rep_in[slot], 64 * (2 * g + p // UQ // 2 + 1))
                    act_fn(dA[p % 2][:, :, lo:hi],
                           REP[:, slot, r, :].rearrange("p (s l) -> p s l", s=SPG)[:, :, lo:hi],
                           ACT.Exp, scale=AR[:, 8 * d + NR * dt + r, k:k + 1]).then_inc(dA_ready, 1)
                    if front:
                        if p == 8:
                            front_xT(f, fp)
                        for q in range(NQ):
                            if p == 10 + 2 * q:
                                front_conv(q, f, fp)
                        if p == 17:
                            silu_u(f, fp)
                        for d_ in range(2):
                            if p == 19 + d_:
                                front_xd(d_, f)
                        for q in range(NQ):
                            if p == 21 + q:
                                front_dt(q, f)
                            if p == 26 + q:
                                front_z(q, f, fp)
                        if p == 25:
                            front_soft(f)
                    if back:
                        if p == 23:
                            back_xT(b)
                        for m in range(HT):
                            if p == 25 + m:
                                back_a(m, b)
                    if p == 29:
                        silus(f, fp, b, front, back)
                        if front:
                            front_ln(f)
                    if back:
                        for m in range(HT):
                            if p == 38 + 2 * m:
                                back_h(1, m, b)
                            if p == 48 + 2 * m:
                                back_h(2, m, b)
                        if p == 45:
                            gelu(1, b)
                        if p == 55:
                            gelu(2, b)

            act.wait_ge(w_in, 16 * W_DMAS)
            for j in range(NJ):
                i_ = act_fn(n_ex[DW * j:DW * (j + 1)],
                            n_al[DW * j:DW * (j + 1)].rearrange("p a (k j) -> p a k j", j=NJ)[:, :, :, j], ACT.Exp)
            i_.then_inc(a_exp, 1)
            for n in range(0, NB_W, 2):
                act.wait_ge(w_pe, n + 1)
                act_fn(copies[n], in_bank(n), ACT.Copy).then_inc(w_act, 1)
            act.wait_ge(const_ok, 2)
            act.wait_ge(dprep, len(DVE_SETUP))
            front_xT(0, 0)
            for q in range(NQ):
                front_conv(q, 0, 0)
            silu_u(0, 0)
            for d in range(2):
                front_xd(d, 0)
            for q in range(NQ):
                front_dt(q, 0)
            front_soft(0)
            for q in range(NQ):
                front_z(q, 0, 0)
            silus(0, 0, 0, True, False)
            front_ln(0)
            iteration(0, 0, True, False)
            with act.Fori(0, G // 2 - 1) as i:
                iteration(2 * i + 1, 1, True, True)
                iteration(2 * i + 2, 0, True, True)
            iteration(G - 1, 1, False, True)
            b = G - 1
            back_xT(b)
            for m in range(HT):
                back_a(m, b)
            silus(0, 0, b, False, True)
            for n in (1, 2):
                for m in range(HT):
                    back_h(n, m, b)
                gelu(n, b)

        @block.vector
        def _(dve):
            def done(table, step, g):
                after(dve, table, step, g)

            def stats(src, st, s_):
                for t in range(NT):
                    i_ = nc.vector.bn_stats(st[:, t, :], src[:, t, :])
                i_.then_inc(s_, 1)

            def aggregate(n, st, mv, rs, stage, s_, g):
                for t in range(NT):
                    i_ = nc.vector.bn_aggr(mv[:, t, :], st[:, t, :])
                i_.then_inc(s_, 1)
                done(stage, "aggr" + n, g)
                nc.vector.tensor_scalar(rs[:, 0, :], mv[:, :, 1], EPS, None, ALU.add).then_inc(s_, 1)

            def normalise(dst, src, mv, rs, s_):
                for t in range(NT):
                    i_ = nc.vector.tensor_scalar(dst[:, t, :], src[:, t, :], mv[:, t, 0:1], rs[:, 1, t:t + 1],
                                                 ALU.subtract, ALU.mult)
                i_.then_inc(s_, 1)

            def front_moments(f):
                dve.wait_ge(x_in, 16 * (f + 1))
                stats(XT, STF, dve_front)

            def front_aggregate(f):
                aggregate("", STF, MVF, RSF, "dve_front", dve_front, f)

            def front_norm(f):
                done("pool_front", "rstd", f)
                normalise(XT, XT, MVF, RSF, dve_front)

            def front_series(f):
                done("act_front", "square", f)
                nc.vector.scalar_tensor_tensor(FG[:, :, :], FG[:, :, :], 13.0 / 16, SPB[:, :, :],
                                               ALU.add, ALU.mult).then_inc(dve_front, 1)
                nc.vector.tensor_scalar(big, SPB[:, :, :], SMALL, None, ALU.is_ge).then_inc(dve_front, 1)

            def front_select():
                nc.vector.copy_predicated(FG[:, :, :], big, SPB[:, :, :]).then_inc(dve_front, 1)

            def front_delta(f, par):
                done("dve_front", "select", f)
                nc.vector.scalar_tensor_tensor(SPB[:, :, :], SPA[:, :, :], 0.0, FG[:, :, :],
                                               ALU.max, ALU.add).then_inc(dve_front, 1)
                done("dve_front", "delta", f)
                nc.vector.tensor_tensor(SPA[:, :, :], SPB[:, :, :], U[:, par], ALU.mult).then_inc(dve_front, 1)

            bank0 = GB[0][:, :].rearrange("p (t c) -> p t c", c=C)

            def back_a(b):
                done("pe_back", "combine", b)
                stats(bank0, STB, dve_back)

            def back_ab(b):
                done("pool_back", "rstd_a", b)
                normalise(TA, bank0, MVB, RSB, dve_back)
                done("dve_back", "norm_a", b)
                nc.vector.tensor_tensor(TA[:, :, :], TA[:, :, :], lnw_b, ALU.mult).then_inc(dve_back, 1)
                done("dve_back", "lnw", b)
                nc.vector.tensor_tensor(TA[:, :, :], TA[:, :, :], lnb_b, ALU.add).then_inc(dve_back, 1)
                done("dve_back", "lnb", b)
                stats(TA, STB, dve_back)

            def back_bc(b):
                done("pool_back", "rstd_b", b)
                normalise(TA, TA, MVB, RSB, dve_back)
                done("dve_back", "norm_b", b)
                dve.wait_ge(xres_in, 16 * (b + 1))
                dve.wait_ge(out_done, 16 * (b + 1))
                nc.vector.tensor_tensor(X1[:, :, :], TA[:, :, :], XRES, ALU.add).then_inc(dve_back, 1)
                done("dve_back", "res_b", b)
                stats(X1, STB, dve_back)

            def back_c(b):
                done("pool_back", "rstd_c", b)
                normalise(TA, X1, MVB, RSB, dve_back)

            def back_b(m, b):
                done("pe_back", f"b{m}", b)
                if m == 0:
                    done("act_back", "silu", b)
                nc.vector.scalar_tensor_tensor(FA[:, m, :], GB[m % 2][:, :], s2c[:, m:m + 1], FA[:, m, :],
                                               ALU.mult, ALU.mult).then_inc(dve_back, 1)

            def back_d(b):
                done("pe_back", "w3", b)
                stats(bank0, STB, dve_back)

            def back_end(b):
                done("pool_back", "rstd_d", b)
                normalise(TA, bank0, MVB, RSB, dve_back)
                done("dve_back", "norm_d", b)
                nc.vector.tensor_tensor(X1[:, :, :], TA[:, :, :], X1[:, :, :], ALU.add).then_inc(dve_back, 1)

            def back_aggregate(n, b):
                aggregate("_" + n, STB, MVB, RSB, "dve_back", dve_back, b)

            def gate(q, g, par):
                wait(dve, y_ready, NQ * g + q + 1)
                nc.vector.tensor_tensor(SZ[:, par, q, :], Y[:, :], SZ[:, par, q, :], ALU.mult).then_inc(gated, 1)

            def scan(p, g):
                d = unit(p)[0]
                wait(dve, dA_ready, g * UNITS + p + 1)
                wait(dve, dbu_ready, g * UNITS + p + 1)
                wait(dve, prod_ready, g * UNITS + p - 1)
                a_, b_, h_ = dA[p % 2][:, :, :].rearrange("p s l -> p (s l)"), DB[:, p % NDB, :], HP[p % 2][:, :]
                if d == 1:
                    a_, b_, h_ = a_[:, ::-1], b_[:, ::-1], h_[:, ::-1]
                nc.vector.tensor_tensor_scan(h_, a_, b_, 0.0, ALU.mult, ALU.add).then_inc(scan_done, 1)

            def product(p, g):
                d, dt, k, r = unit(p)
                if p % (2 * UQ) == 0:
                    dve.wait_ge(bc_in[d], 64 * (g + 1))
                if p % NR == 0:
                    wait(dve, sums_done, UNITS // NR * g + p // NR - 1)
                wait(dve, scan_done, g * UNITS + p + 1)
                nc.vector.tensor_tensor(PR[:, (p // NR) % 2, r, :], HP[p % 2][:, :], BC[:, d, NK + k, :],
                                        ALU.mult).then_inc(prod_ready, 1)

            def iteration(g, par, front, back):
                f, b, fp = g + 1, g - 1, 1 - par
                for p in range(UNITS):
                    if front and p == 3:
                        done("dve_front", "stats", f)
                    if front and p == 32:
                        done("dve_front", "large", f)
                        done("act_front", "ln", f)
                    if back:
                        for n, at in STATS_AT:
                            if p == at + 1:
                                done("dve_back", "stats_" + n, b)
                    scan(p, g)
                    if p > 0:
                        product(p - 1, g)
                    for q in range(NQ - 1):
                        if p == UQ * (q + 1) + 2:
                            gate(q, g, par)
                    if back:
                        if p == 1:
                            gate(NQ - 1, b, fp)
                    if front:
                        if p == 2:
                            front_moments(f)
                        if p == 3:
                            front_aggregate(f)
                        if p == 6:
                            front_norm(f)
                        if p == 27:
                            front_series(f)
                        if p == 32:
                            front_select()
                            front_delta(f, fp)
                    if back:
                        for n, at in STATS_AT:
                            if p == at + 1:
                                back_aggregate(n, b)
                        if p == 7:
                            back_a(b)
                        if p == 11:
                            back_ab(b)
                        if p == 15:
                            back_bc(b)
                        if p == 19:
                            back_c(b)
                        for m in range(HT):
                            if p == 31 + m:
                                back_b(m, b)
                        if p == 59:
                            back_d(b)
                product(UNITS - 1, g)
                if back:
                    back_end(b)

            STATS_AT = (("a", 7), ("b", 11), ("c", 15), ("d", 59))

            def broadcast(v):
                return v[:, :].rearrange("p (a c) -> p a c", a=1).to_broadcast([128, NT, C])

            lnw_b, lnb_b = broadcast(lnw), broadcast(lnb)

            dve.wait_ge(w_in, 16 * W_DMAS)
            for d in range(2):
                for t in range(DT):
                    for k in range(TAPS):
                        q = d * DT + t
                        nc.vector.tensor_scalar(n_tap[:, q * TAPS + k, :], n_in[:, 4 * d + t, :],
                                                cw[:, q, k:k + 1], None, ALU.mult)
            nc.vector.tensor_scalar(n_w3s, n_w3, w3c[:, 0:1], None, ALU.mult).then_inc(dprep, 1)
            dve.wait_ge(const_ok, 2)
            nc.vector.tensor_reduce(fold[:, :], ident[:, :].rearrange("p (j d) -> p d j", d=DW), op=ALU.add,
                                    axis=AX.X).then_inc(dprep, 1)
            for q in range(NQ):
                i_ = nc.vector.tensor_scalar(DD[:, q, :], ident[:, :], dp[:, q:q + 1], None, ALU.mult)
            i_.then_inc(dprep, 1)
            dve.wait_ge(a_exp, 1)
            nc.vector.tensor_scalar(AR[:, :, :], n_ex, -1.0, None, ALU.mult).then_inc(dprep, 1)
            for n in range(1, NB_W, 2):
                dve.wait_ge(w_pe, n + 1)
                nc.vector.tensor_copy(copies[n], in_bank(n)).then_inc(w_dve, 1)
            dve.wait_ge(w_dve, N_PT // 2 + 1)
            nc.vector.tensor_tensor(P12[:, :], PT[:, 0, :], PT[:, 1, :], ALU.add).then_inc(dprep, 1)
            front_moments(0)
            done("dve_front", "stats", 0)
            front_aggregate(0)
            front_norm(0)
            front_series(0)
            done("act_front", "ln", 0)
            done("dve_front", "large", 0)
            front_select()
            front_delta(0, 0)
            iteration(0, 0, True, False)
            with dve.Fori(0, G // 2 - 1) as i:
                iteration(2 * i + 1, 1, True, True)
                iteration(2 * i + 2, 0, True, True)
            iteration(G - 1, 1, False, True)
            b = G - 1
            gate(NQ - 1, b, 1)
            back_a(b)
            done("dve_back", "stats_a", b)
            back_aggregate("a", b)
            back_ab(b)
            done("dve_back", "stats_b", b)
            back_aggregate("b", b)
            back_bc(b)
            done("dve_back", "stats_c", b)
            back_aggregate("c", b)
            back_c(b)
            for m in range(HT):
                back_b(m, b)
            back_d(b)
            done("dve_back", "stats_d", b)
            back_aggregate("d", b)
            back_end(b)

        @block.tensor
        def _(pe):
            mm = nc.tensor.matmul

            def done(table, step, g):
                after(pe, table, step, g)

            def front_bank(step, f):
                steps = [s_ for s_ in ACT_FRONT if s_ in PE_FRONT]
                at = steps.index(step)
                done("act_front", steps[at - 1], f) if at else done("act_front", steps[-1], f - 1)

            def front_xT(f):
                front_bank("xT", f)
                done("dve_front", "norm", f)
                for t in range(NT):
                    i_ = nc.tensor.transpose(GF[:, 128 * t:128 * (t + 1)], XT[:, t, :], ident[:, :])
                i_.then_inc(pe_front, 1)

            def front_conv(q, f, par):
                d, t = q // DT, q % DT
                front_bank(f"conv{q}", f)
                for k in range(TAPS):
                    at = k if d == 0 else 2 * PAD - k
                    i_ = mm(GF[:, :], tapT[:, d, k, 128 * t:128 * (t + 1)], XNT[:, par, :, at:at + L],
                            start=(k == 0), stop=(k == TAPS - 1))
                i_.then_inc(pe_front, 1)

            def front_z(q, f, par):
                front_bank(f"z{q}", f)
                mm(GF[:, :], zT[:, q, :], XNT[:, par, :, PAD:PAD + L], start=True, stop=True).then_inc(pe_front, 1)

            def front_xd(d, f, par):
                if d == 0:
                    done("act_front", "silu_u", f)
                front_bank(f"xd{d}", f)
                for t in range(DT):
                    i_ = mm(GF[0:RANK + 2 * NS, :], xpT[:, d * DT + t, :], U[:, par, d * DT + t, :],
                            start=(t == 0), stop=(t == DT - 1))
                i_.then_inc(pe_front, 1)

            def front_dt(q, f):
                front_bank(f"dt{q}", f)
                mm(GF[:, :], dtT[:, q, :], XD[0:RANK, q // DT, :], start=True, stop=True).then_inc(pe_front, 1)

            def combine(b, par):
                wait(pe, gated, NQ * (b + 1))
                for t in range(NT):
                    o = GB[0][:, C * t:C * (t + 1)]
                    tok = slice(128 * t, 128 * (t + 1))
                    for q in range(NQ):
                        mm(o, SZ[:, par, q, tok], WE[:, q, :], start=(q == 0), stop=False)
                    s_, h_ = t * 128 // L, t * 128 % L
                    mm(o, XNT[:, par, s_, PAD + h_:PAD + h_ + 128], P12[:, :], start=False, stop=False)
                    i_ = mm(o, ones[:, :], pbrow[:, :], start=False, stop=True)
                i_.then_inc(pe_back, 1)

            def back_xT(b):
                done("dve_back", "norm_c", b)
                for t in range(NT):
                    i_ = nc.tensor.transpose(GB[1][:, 128 * t:128 * (t + 1)], TA[:, t, :], ident[:, :])
                i_.then_inc(pe_back, 1)

            def back_up(n, m, b):
                w = {"a": w1T, "b": w2T}[n]
                if n == "a":
                    done("act_back", "xT", b)
                    done("dve_back", "norm_a", b) if m == 0 else None
                    done("act_back", f"a{m - 2}", b) if m >= 2 else None
                else:
                    done("act_back", f"a{m + 2}", b) if m < 2 else done("dve_back", f"b{m - 2}", b)
                mm(GB[m % 2][:, :], w[:, 128 * m:128 * (m + 1)], X2T[:, :], start=True, stop=True).then_inc(pe_back, 1)

            def back_h(n, m, b):
                w, src = ((h1T, FA), (h2T, FG))[n - 1]
                if n == 1:
                    done("dve_back", f"b{HT - 1}", b)
                else:
                    done("act_back", "gelu1", b)
                if m >= 2:
                    done("act_back", f"h{n}_{m - 2}", b)
                for k in range(HT):
                    i_ = mm(GB[m % 2][:, :], w[:, k, 128 * m:128 * (m + 1)], src[:, k, :],
                            start=(k == 0), stop=(k == HT - 1))
                i_.then_inc(pe_back, 1)

            def back_w3(b):
                done("act_back", "gelu2", b)
                for t in range(NT):
                    for k in range(HT):
                        i_ = mm(GB[0][:, C * t:C * (t + 1)], FA[:, k, 128 * t:128 * (t + 1)], w3T[:, k, :],
                                start=(k == 0), stop=(k == HT - 1))
                i_.then_inc(pe_back, 1)

            def sums(s_, g, par):
                q = s_ * NR // UQ
                last = s_ % NK == NK - 1
                if s_ % NK == 0:
                    wait(pe, gated, NQ * g + q)
                    mm(Y[:, :], DD[:, q, :], U[:, par, q, :], start=True, stop=False)
                wait(pe, prod_ready, g * UNITS + NR * (s_ + 1))
                for r in range(NR):
                    i_ = mm(Y[DW * r:DW * (r + 1), :], fold[:, :], PR[:, s_ % 2, r, :], start=False, stop=last)
                i_.then_inc(sums_done, 1)
                if last:
                    pe.wait_ge(sums_done, UNITS // NR * g + s_ + 1)
                    pe.sem_inc(y_ready, 1)

            def iteration(g, par, front, back):
                f, b, fp = g + 1, g - 1, 1 - par
                for p in range(UNITS):
                    if p % NR == 1 and p > NR:
                        sums(p // NR - 1, g, par)
                    if back and p == 3:
                        combine(b, fp)
                    if front:
                        if p == 7:
                            front_xT(f)
                        for q in range(NQ):
                            if p == 8 + 2 * q:
                                front_conv(q, f, fp)
                        for d in range(2):
                            if p == 18 + d:
                                front_xd(d, f, fp)
                        for q in range(NQ):
                            if p == 20 + q:
                                front_dt(q, f)
                            if p == 25 + q:
                                front_z(q, f, fp)
                    if back:
                        if p == 22:
                            back_xT(b)
                        for m in range(HT):
                            if p == 24 + m:
                                back_up("a", m, b)
                    if back:
                        for m in range(HT):
                            if p == 30 + m:
                                back_up("b", m, b)
                    if back:
                        for m in range(HT):
                            if p == 36 + 2 * m:
                                back_h(1, m, b)
                            if p == 46 + 2 * m:
                                back_h(2, m, b)
                        if p == 57:
                            back_w3(b)
                sums(UNITS // NR - 1, g, par)

            pe.wait_ge(w_in, 16 * W_DMAS)
            pe.wait_ge(const_ok, 2)
            pe.wait_ge(dprep, DVE_SETUP.index("scaled") + 1)
            for n in range(NB_W):
                if n >= 2:
                    pe.wait_ge((w_act, w_dve)[n % 2], n // 2)
                o = in_bank(n)
                if n == N_H:
                    pe.wait_ge(w_in2, 32)
                if n == N_WE:
                    pe.wait_ge((w_act, w_dve)[N_PT % 2], N_PT // 2 + 1)
                    for q in range(NQ):
                        i_ = mm(o[:, q, :], n_out[:, q, :], PT[:, q // DT, :], start=True, stop=True)
                else:
                    for a, src in enumerate(batches[n][0]):
                        rows = src.shape[0]
                        i_ = nc.tensor.transpose(o[:, a, :], src, ident[0:rows, 0:rows])
                i_.then_inc(w_pe, 1)
            pe.wait_ge(w_act, (NB_W + 1) // 2)
            pe.wait_ge(dprep, len(DVE_SETUP))
            front_xT(0)
            for q in range(NQ):
                front_conv(q, 0, 0)
            for d in range(2):
                front_xd(d, 0, 0)
            for q in range(NQ):
                front_dt(q, 0)
            for q in range(NQ):
                front_z(q, 0, 0)
            iteration(0, 0, True, False)
            with pe.Fori(0, G // 2 - 1) as i:
                iteration(2 * i + 1, 1, True, True)
                iteration(2 * i + 2, 0, True, True)
            iteration(G - 1, 1, False, True)
            b = G - 1
            combine(b, 1)
            back_xT(b)
            for n in "ab":
                for m in range(HT):
                    back_up(n, m, b)
            for n in (1, 2):
                for m in range(HT):
                    back_h(n, m, b)
            back_w3(b)


MAMBA_NAMES = ["in_w", "conv_w", "conv_b", "xproj_w", "dt_w", "dt_b", "Alog", "Dp", "out_w"]
_INS = ["L0_attn_x"] + [f"L0_attn_{d}_{n}" for d in ("fw", "bw") for n in MAMBA_NAMES] \
    + ["L0_attn_proj_w", "L0_attn_proj_b", "L0_attn_ln_w", "L0_attn_ln_b"] \
    + [f"L0_ffn_{n}" for n in ("w1_w", "w1_s", "w2_w", "w2_s", "h1_w", "h1_s", "h2_w", "h2_s", "w3_w", "w3_s")]


def kernel(**inputs):
    import numpy as _np
    import concourse.bacc as _bacc
    from concourse import mybir as _mybir
    from concourse.bass_utils import run_bass_kernel_spmd as _run

    nc = _bacc.Bacc("TRN2", target_bir_lowering=False, num_devices=1)
    arrays, args = {}, {}
    for name in _INS:
        a = _np.ascontiguousarray(inputs[name])
        arrays[f"in_{name}_dram"] = a
        args[name] = nc.dram_tensor(f"in_{name}_dram", a.shape, _mybir.dt.from_np(a.dtype), kind="ExternalInput").ap()
    out = nc.dram_tensor("out_0_dram", (SEQS, L, C), _mybir.dt.float32, kind="ExternalOutput").ap()
    fw, bw = ({n: args[f"L0_attn_{d}_{n}"] for n in MAMBA_NAMES} for d in ("fw", "bw"))
    rest = [args[n] for n in _INS[1 + 2 * len(MAMBA_NAMES):]]
    build(nc, args["L0_attn_x"], fw, bw, *rest, out)
    r = _run(nc, [arrays], core_ids=[0])
    return r.results[0]["out_0_dram"]
```

```python
import concourse.bass as bass
from concourse import mybir
from contextlib import ExitStack

SEQS, L, C = 16, 256, 128
DI, NS, RANK, TAPS = 256, 16, 8, 4
HID = 512
SPG = 2
T = SPG * L
G = SEQS // SPG
NT = T // 128
DT = DI // 128
NQ = 2 * DT
NJ, DW = 4, 32
NK = NS // NJ
NR = 128 // DW
UNITS = NQ * NK * NR
UQ = NK * NR
PAD = TAPS - 1
LP = L + 2 * PAD
HT = HID // 128
EPS = 1e-5
SMALL = 2.0 ** -7
NDB = 4

SOFT = [(n, s - i) for s in range(NQ + 2) for i, n in enumerate(("abs", "exp", "square")) if 0 <= s - i < NQ]
SOFT_STEPS = NQ + 2


def each(name, n):
    return [f"{name}{i}" for i in range(n)]


PE_FRONT = ["xT"] + each("conv", NQ) + each("xd", 2) + each("dt", NQ) + each("z", NQ)
ACT_FRONT = ["xT"] + each("conv", NQ) + each("silu_u", NQ) + each("xd", 2) + each("dt", NQ) \
    + [f"{n}{q}" for n, q in SOFT] + each("z", NQ) + each("silu_z", NQ) + each("ln", NQ)
DVE_FRONT = ["stats", "aggr", "var", "norm"] + [f"{n}{q}" for q in range(NQ) for n in ("series", "large")] \
    + [f"{n}{q}" for q in range(NQ) for n in ("select", "delta")]
POOL_FRONT = ["rstd"] + each("du", NQ)
PE_BACK = ["combine", "xT"] + each("a", HT) + each("b", HT) + each("h1_", HT) + each("h2_", HT) + ["w3"]
ACT_BACK = ["xT"] + each("a", HT) + each("silu", HT) + each("h1_", HT) + each("gelu1_", HT) \
    + each("h2_", HT) + each("gelu2_", HT)
DVE_BACK = ["stats_a", "aggr_a", "var_a", "norm_a", "stats_b", "aggr_b", "var_b", "norm_b",
            "stats_c", "aggr_c", "var_c", "norm_c"] + each("b", HT) + ["stats_d", "aggr_d", "var_d", "norm_d"]
POOL_BACK = ["rstd_a", "lnw", "lnb", "rstd_b", "res_b", "rstd_c", "rstd_d", "res_d"]
PE_TAIL = PE_BACK
ACT_TAIL = ["xT"] + each("a", HT) + each("h1_", HT) + each("h2_", HT)

AT = {
    "pe_combine": [3], "pe_xT": [7], "pe_conv": [8, 10, 12, 14], "pe_xd": [18, 19], "pe_dt": [20, 21, 22, 23],
    "pe_z": [28, 29, 30, 31], "pe_bxT": [22], "pe_a": [24, 25, 26, 27], "pe_b": [30, 31, 32, 33],
    "pe_h1": [36, 38, 40, 42], "pe_h2": [46, 48, 50, 52], "pe_w3": [57],
    "act_xT": [8], "act_conv": [10, 12, 14, 16], "act_silu_u": [17, 17, 17, 17], "act_xd": [19, 20],
    "act_dt": [21, 22, 23, 24], "act_soft": [24, 25, 26, 27, 28, 29], "act_z": [29, 30, 31, 32],
    "act_silu_z": [32, 32, 32, 32], "act_ln": [33, 34, 35, 36], "act_bxT": [23], "act_a": [25, 26, 27, 28],
    "act_silu_a": [29, 29, 29, 29], "act_h1": [38, 40, 42, 44], "act_gelu1": [45, 45, 45, 45],
    "act_h2": [48, 50, 52, 54], "act_gelu2": [55, 55, 55, 55],
    "pool_rstd": [4], "pool_a": [9], "pool_ln": [11, 12], "pool_b": [14], "pool_res_b": [16], "pool_c": [18],
    "pool_d": [61], "pool_du": [36, 37, 38, 39],
    "dve_stats": [2], "dve_norm": [6], "dve_gate": [18, 34, 50], "dve_last_gate": [1],
    "dve_series": [27, 28, 29, 30], "dve_select": [34, 35, 36, 37],
    "dve_a": [7], "dve_norm_a": [10], "dve_b": [13], "dve_norm_b": [15], "dve_c": [17], "dve_norm_c": [19],
    "dve_mul": [31, 32, 33, 34], "dve_d": [59],
    "pe_sums": [1],
}


def at(name, p):
    return [i for i, unit_ in enumerate(AT[name]) if unit_ == p]


def build(nc, x, w, out):
    f32 = mybir.dt.float32
    ALU, ACT, AX = mybir.AluOpType, mybir.ActivationFunctionType, mybir.AxisListType

    dd = nc.dram_tensor("delta_and_du", (2, NQ, 2, 128, T), f32).ap()
    bc = nc.dram_tensor("b_and_c", (2, 2, 2 * NS, T), f32).ap()
    x_g = x.rearrange("(g s) (h p) c -> g p (s h) c", s=SPG, p=128)
    out_g = out.rearrange("(g s) (h p) c -> g p (s h) c", s=SPG, p=128)

    with ExitStack() as ctx:
        def sb(name, shape):
            return ctx.enter_context(nc.sbuf_tensor(name, shape, f32))

        def pb(name, shape=(128, T)):
            return ctx.enter_context(nc.psum_tensor(name, list(shape), f32))

        def sem(name):
            return ctx.enter_context(nc.semaphore(name))

        REP = sb("rep", [128, 2, 2 * NR, T])
        BC = sb("bc_rep", [128, 2, 2 * NK, T])
        DB = sb("dbu", [128, NDB, T])
        PR = sb("prod", [128, 2, NR, T])
        AR = sb("a_rep", [128, 2 * 8, NK])
        XT = sb("x_tok", [128, NT, C])
        XNT = sb("xn_t", [128, 2, SPG, LP])
        U = sb("u", [128, 2, NQ, T])
        SZ = sb("silu_z", [128, 2, NQ, T])
        SPA = sb("dt_raw", [128, NQ, T])
        SPB = sb("delta", [128, NQ, T])
        TA = sb("normed", [128, NT, C])
        X1 = sb("x1", [128, NT, C])
        X2T = sb("x2_t", [128, T])
        XRES = X2T[:, :].rearrange("p (t c) -> p t c", c=C)
        FA = sb("ffn_a", [128, HT, T])
        FG = sb("ffn_g", [128, HT, T])
        XD = FG[0:RANK + 2 * NS, 0:2, :]
        STF, MVF, RSF = sb("stf", [128, NT, 6]), sb("mvf", [128, NT, 2]), sb("rsf", [128, 2, NT])
        STB, MVB, RSB = sb("stb", [128, NT, 6]), sb("mvb", [128, NT, 2]), sb("rsb", [128, 2, NT])
        ident = sb("ident", [128, 128])
        fold = sb("fold", [128, DW])
        mhalf = sb("minus_half", [128, NT])
        zero2 = sb("zero2", [128, SPG])
        ones = sb("ones", [1, 128])
        pbrow = sb("proj_b_row", [1, C])
        lnw, lnb = sb("lnw", [128, C]), sb("lnb", [128, C])
        tapT = sb("tap_t", [128, 2, TAPS, DI])
        zT = sb("z_t", [128, NQ, 128])
        xpT = sb("xproj_t", [128, NQ, RANK + 2 * NS])
        dtT = sb("dt_t", [RANK, NQ, 128])
        P12 = sb("proj_sum_t", [128, 128])
        WE = sb("w_eff", [128, NQ, C])
        DD = sb("d_diag", [128, NQ, 128])
        w1T, w2T = sb("w1_t", [128, HID]), sb("w2_t", [128, HID])
        h1T, h2T = sb("h1_t", [128, HT, HID]), sb("h2_t", [128, HT, HID])
        w3T = sb("w3_t", [128, HT, C])
        cols = sb("columns", [128, 3 * NQ + 4 * HT])
        cb, db, dp = (cols[:, NQ * i:NQ * (i + 1)] for i in range(3))
        s1c, s2c, h1c, h2c = (cols[:, 3 * NQ + HT * i:3 * NQ + HT * (i + 1)] for i in range(4))
        root = sb("minus_root", [128, 1])
        big = TA[:, :, :].rearrange("p t c -> p (t c)").bitcast(mybir.dt.uint8) \
            .rearrange("p (q l) -> p q l", q=NQ)
        n_in = REP[:, 1, 0, :].rearrange("p (d c) -> p d c", d=2)
        n_out = REP[:, 1, 1, :].rearrange("p (q c) -> p q c", c=128)
        PT = REP[:, 1, 2, 0:2 * C].rearrange("p (d c) -> p d c", d=2)
        w3row = REP[:, 1, 3, 0:C]

        dA = [pb(f"dA{i}", (128, SPG, L)) for i in range(2)]
        HP = [pb(f"h{i}") for i in range(2)]
        Y = pb("y")
        GF = pb("front_bank")
        GB = [pb(f"back_bank{i}") for i in range(2)]

        w_conv = sem("w_conv")
        w_front = sem("w_front")
        w_comb = sem("w_comb")
        w_back = sem("w_back")
        const_ok = sem("const_ok")
        dprep = sem("dprep")
        we_pe, we_act = sem("we_pe"), sem("we_act")
        a_exp = sem("a_exp")
        dA_ready, dbu_ready = sem("dA_ready"), sem("dbu_ready")
        scan_done, prod_ready = sem("scan_done"), sem("prod_ready")
        zero_set = sem("zero_set")
        sums_done = sem("sums_done")
        y_ready, gated = sem("y_ready"), sem("gated")
        rep_in = [sem("rep_in0"), sem("rep_in1")]
        bc_in = [sem("bc_in0"), sem("bc_in1")]
        x_in, xres_in, out_done = sem("x_in"), sem("xres_in"), sem("out_done")
        bc_out, dd_out = sem("bc_out"), [sem(f"dd_out{q}") for q in range(NQ)]
        pe_front, act_front, dve_front, pool_front = (sem(n) for n in ("pe_front", "act_front", "dve_front", "pool_front"))
        pe_back, act_back, dve_back, pool_back = (sem(n) for n in ("pe_back", "act_back", "dve_back", "pool_back"))

        pe_tail, act_tail = sem("pe_tail"), sem("act_tail")

        TABLES = {"pe_front": (pe_front, PE_FRONT), "act_front": (act_front, ACT_FRONT),
                  "dve_front": (dve_front, DVE_FRONT), "pool_front": (pool_front, POOL_FRONT),
                  "pe_back": (pe_back, PE_BACK), "act_back": (act_back, ACT_BACK),
                  "dve_back": (dve_back, DVE_BACK), "pool_back": (pool_back, POOL_BACK),
                  "pe_tail": (pe_tail, PE_TAIL), "act_tail": (act_tail, ACT_TAIL)}

        def wait(eng, s, value):
            if not isinstance(value, int) or value > 0:
                eng.wait_ge(s, value)

        def after(eng, table, step, g):
            s, steps = TABLES[table]
            if isinstance(g, int) and g < 0:
                return
            wait(eng, s, g * len(steps) + steps.index(step) + 1)

        def unit(p):
            q = p // UQ
            return q // DT, q % DT, (p % UQ) // NR, p % NR

        DVE_SETUP = each("tap", NQ) + ["fold", "d_diag", "a_rep", "p12", "w3"]
        N_CONV, N_FRONT, N_COMB, N_BACK = 3, 4, 2, 9
        SET1 = [dA[0][:, :, :].rearrange("p s l -> p (s l)"), dA[1][:, :, :].rearrange("p s l -> p (s l)"),
                HP[0][:, :], HP[1][:, :]]
        SET2 = [Y[:, :], GB[0][:, :], GB[1][:, :], GF[:, :]]

        block = ctx.enter_context(nc.Block())

        @block.sync
        def _(sp):
            def rep_load(q, g, par, slot):
                for j in range(NJ):
                    sp.dma_start(REP[DW * j:DW * (j + 1), slot, :, :],
                                 dd[par, q].rearrange("t (r p) l -> p (t r) l", p=DW)).then_inc(rep_in[slot], 16)

            def bc_load(d, g, par):
                for j in range(NJ):
                    rows = bc[par, d].rearrange("(m j) l -> j m l", j=NJ)[j:j + 1]
                    sp.dma_start(BC[DW * j:DW * (j + 1), d, :, :],
                                 rows.to_broadcast([DW, 2 * NK, T])).then_inc(bc_in[d], 16)

            def half_free(q, g):
                wait(sp, dA_ready, g * UNITS + UQ * (q + 1))
                wait(sp, dbu_ready, g * UNITS + UQ * (q + 1))

            def bc_free(d, g):
                wait(sp, dbu_ready, g * UNITS + 2 * UQ * (d + 1))
                wait(sp, prod_ready, g * UNITS + 2 * UQ * (d + 1))

            def bc_store(f, par):
                if not (isinstance(f, int) and f < 2):
                    wait(sp, bc_in[0], (f - 1) * 64)
                    wait(sp, bc_in[1], (f - 1) * 64)
                for d in range(2):
                    after(sp, "act_front", f"xd{d}", f)
                    sp.dma_start(bc[par, d], XD[RANK:RANK + 2 * NS, d, :]).then_inc(bc_out, 16)

            def dd_store(f, par):
                if not (isinstance(f, int) and f < 2):
                    wait(sp, rep_in[0], (f - 1) * 128)
                    wait(sp, rep_in[1], (f - 1) * 128)
                for q in range(NQ):
                    after(sp, "dve_front", f"delta{q}", f)
                    sp.dma_start(dd[par, q, 0], SPB[:, q, :]).then_inc(dd_out[q], 16)
                    after(sp, "pool_front", f"du{q}", f)
                    sp.dma_start(dd[par, q, 1], SPA[:, q, :]).then_inc(dd_out[q], 16)

            def iteration(g, par, front, back):
                f, b = g + 1, g - 1
                fp = 1 - par
                if front:
                    after(sp, "pe_front", "xT", f - 1)
                    sp.dma_start(XT[:, :, :], x_g[f]).then_inc(x_in, 16)
                if back:
                    sp.dma_start(XRES, x_g[b]).then_inc(xres_in, 16)
                half_free(3, g - 1)
                rep_load(1, g, par, 1)
                bc_free(1, g - 1)
                bc_load(1, g, par)
                half_free(0, g)
                rep_load(2, g, par, 0)
                if front:
                    bc_store(f, fp)
                half_free(1, g)
                rep_load(3, g, par, 1)
                if front:
                    bc_free(0, g)
                    wait(sp, bc_out, (f + 1) * 32)
                    bc_load(0, f, fp)
                    dd_store(f, fp)
                    half_free(2, g)
                    for q in range(NQ):
                        wait(sp, dd_out[q], (f + 1) * 32)
                    rep_load(0, f, fp, 0)
                if back:
                    after(sp, "pool_back", "res_d", b)
                    sp.dma_start(out_g[b], X1[:, :, :]).then_inc(out_done, 16)

            def load(dst, name, s_):
                sp.dma_start(dst, w[name]).then_inc(s_, 16)

            def load_row(dst, name, shape, s_):
                sp.dma_start(dst, w[name].to_broadcast(shape)).then_inc(s_, 16)

            sp.dma_start(XT[:, :, :], x_g[0]).then_inc(x_in, 16)
            sp.dma_start(n_in, w["in_t"][:, :, 0:DI]).then_inc(w_conv, 16)
            load_row(tapT[:, :, :, :].rearrange("p d k c -> p (d k c)"), "taps", [128, 2 * TAPS * DI], w_conv)
            load(cols[:, :], "columns", w_conv)
            load(xpT[:, :, :], "xproj_t", w_front)
            load(dtT[:, :, :], "dt_t", w_front)
            sp.dma_start(zT[:, :, :].rearrange("p (d t) c -> p d (t c)", d=2), w["in_t"][:, :, DI:2 * DI]).then_inc(w_front, 16)
            load(AR[:, :, :], "a_log", w_front)
            load(n_out, "out_w", w_comb)
            load(PT, "proj_t", w_comb)
            load(pbrow[:, :], "proj_b", w_back)
            load_row(lnw[:, :], "ln_w", [128, C], w_back)
            load_row(lnb[:, :], "ln_b", [128, C], w_back)
            load_row(w3row, "w3_s", [128, C], w_back)
            for dst, name in ((w3T, "w3_t"), (h1T, "h1_t"), (h2T, "h2_t")):
                load(dst[:, :, :], name, w_back)
            for dst, name in ((w1T, "w1_t"), (w2T, "w2_t")):
                load(dst[:, :], name, w_back)

            sp.sem_inc(out_done, 16)
            bc_store(0, 0)
            wait(sp, bc_out, 32)
            bc_load(0, 0, 0)
            dd_store(0, 0)
            wait(sp, dd_out[0], 32)
            rep_load(0, 0, 0, 0)
            for q in range(1, NQ):
                wait(sp, dd_out[q], 32)
            sp.wait_ge(we_act, 1)
            sp.wait_ge(dprep, len(DVE_SETUP))

            iteration(0, 0, True, False)
            with sp.Fori(0, G // 2 - 1) as i:
                iteration(2 * i + 1, 1, True, True)
                iteration(2 * i + 2, 0, True, True)
            iteration(G - 1, 1, False, True)
            sp.dma_start(XRES, x_g[G - 1]).then_inc(xres_in, 16)
            after(sp, "pool_back", "res_d", G - 1)
            sp.dma_start(out_g[G - 1], X1[:, :, :]).then_inc(out_done, 16)
            sp.wait_ge(out_done, 16 * (G + 1))

        @block.gpsimd
        def _(pool):
            def rstd_front(f):
                after(pool, "dve_front", "var", f)
                nc.gpsimd.tensor_tensor(RSF[:, 1, :], RSF[:, 0, :], mhalf[:, :], ALU.pow).then_inc(pool_front, 1)

            def rstd_back(n, b):
                after(pool, "dve_back", "var_" + n, b)
                nc.gpsimd.tensor_tensor(RSB[:, 1, :], RSB[:, 0, :], mhalf[:, :], ALU.pow).then_inc(pool_back, 1)

            def broadcast(v):
                return v[:, :].rearrange("p (a c) -> p a c", a=1).to_broadcast([128, NT, C])

            def times_lnw(b):
                after(pool, "dve_back", "norm_a", b)
                nc.gpsimd.tensor_tensor(TA[:, :, :], TA[:, :, :], broadcast(lnw), ALU.mult).then_inc(pool_back, 1)

            def plus_lnb(b):
                after(pool, "pool_back", "lnw", b)
                nc.gpsimd.tensor_tensor(TA[:, :, :], TA[:, :, :], broadcast(lnb), ALU.add).then_inc(pool_back, 1)

            def residual_b(b):
                after(pool, "dve_back", "norm_b", b)
                pool.wait_ge(xres_in, 16 * (b + 1))
                pool.wait_ge(out_done, 16 * (b + 1))
                nc.gpsimd.tensor_tensor(X1[:, :, :], TA[:, :, :], XRES, ALU.add).then_inc(pool_back, 1)

            def residual_d(b):
                after(pool, "dve_back", "norm_d", b)
                nc.gpsimd.tensor_tensor(X1[:, :, :], TA[:, :, :], X1[:, :, :], ALU.add).then_inc(pool_back, 1)

            def front_du(q, f, par):
                after(pool, "dve_front", f"delta{q}", f)
                nc.gpsimd.tensor_tensor(SPA[:, q, :], SPB[:, q, :], U[:, par, q, :], ALU.mult).then_inc(pool_front, 1)

            def iteration(g, par, front, back):
                f, b, fp = g + 1, g - 1, 1 - par
                for p in range(UNITS):
                    d, dt, k, r = unit(p)
                    slot = (p // UQ) % 2
                    if p % UQ == 0:
                        pool.wait_ge(rep_in[slot], 64 * (2 * g + p // UQ // 2 + 1))
                    if p % (2 * UQ) == 0:
                        pool.wait_ge(bc_in[d], 64 * (g + 1))
                    wait(pool, scan_done, g * UNITS + p - NDB + 1)
                    nc.gpsimd.tensor_tensor(DB[:, p % NDB, :], REP[:, slot, NR + r, :], BC[:, d, k, :],
                                            ALU.mult).then_inc(dbu_ready, 1)
                    if front:
                        for _ in at("pool_rstd", p):
                            rstd_front(f)
                        for q in at("pool_du", p):
                            front_du(q, f, fp)
                    if back:
                        for _ in at("pool_a", p):
                            rstd_back("a", b)
                        for i in at("pool_ln", p):
                            (times_lnw, plus_lnb)[i](b)
                        for _ in at("pool_b", p):
                            rstd_back("b", b)
                        for _ in at("pool_res_b", p):
                            residual_b(b)
                        for _ in at("pool_c", p):
                            rstd_back("c", b)
                        for _ in at("pool_d", p):
                            rstd_back("d", b)
                if back:
                    residual_d(b)

            nc.gpsimd.memset(ident[:, :], 0.0).then_inc(const_ok, 1)
            nc.gpsimd.memset(mhalf[:, :], -0.5)
            nc.gpsimd.memset(zero2[:, :], 0.0)
            nc.gpsimd.memset(root[:, :], -(3.0 ** 0.5) / 4)
            nc.gpsimd.memset(ones[:, :], 1.0)
            nc.gpsimd.memset(XNT[:, :, :, :], 0.0)
            pool.wait_ge(const_ok, 1)
            nc.gpsimd.affine_select(out=ident[:, :], in_=ident[:, :], compare_op=ALU.not_equal, fill=1.0,
                                    base=0, pattern=[[-1, 128]], channel_multiplier=1).then_inc(const_ok, 1)
            pool.wait_ge(const_ok, 2)
            rstd_front(0)
            for q in range(NQ):
                front_du(q, 0, 0)
            pool.wait_ge(w_back, 16 * N_BACK)
            iteration(0, 0, True, False)
            with pool.Fori(0, G // 2 - 1) as i:
                iteration(2 * i + 1, 1, True, True)
                iteration(2 * i + 2, 0, True, True)
            iteration(G - 1, 1, False, True)
            b = G - 1
            rstd_back("a", b)
            times_lnw(b)
            plus_lnb(b)
            rstd_back("b", b)
            residual_b(b)
            rstd_back("c", b)
            rstd_back("d", b)
            residual_d(b)

        @block.scalar
        def _(act):
            act_fn = nc.scalar.activation

            def front_xT(f, par):
                after(act, "pe_front", "xT", f)
                after(act, "pe_back", "combine", f - 2)
                act_fn(XNT[:, par, :, PAD:PAD + L], GF[:, :].rearrange("p (s l) -> p s l", s=SPG),
                       ACT.Copy).then_inc(act_front, 1)

            def front_conv(q, f, par):
                after(act, "pe_front", f"conv{q}", f)
                act_fn(U[:, par, q, :], GF[:, :], ACT.Identity, bias=cb[:, q:q + 1]).then_inc(act_front, 1)

            def front_z(q, f, par):
                after(act, "pe_front", f"z{q}", f)
                act_fn(SZ[:, par, q, :], GF[:, :], ACT.Copy).then_inc(act_front, 1)

            def silu_u(q, f, par):
                after(act, "act_front", f"conv{q}", f)
                act_fn(U[:, par, q, :], U[:, par, q, :], ACT.Silu).then_inc(act_front, 1)

            def silu_z(q, f, par):
                after(act, "act_front", f"z{q}", f)
                act_fn(SZ[:, par, q, :], SZ[:, par, q, :], ACT.Silu).then_inc(act_front, 1)

            def silu_a(m, b):
                after(act, "act_back", f"a{m}", b)
                act_fn(FA[:, m, :], FA[:, m, :], ACT.Silu).then_inc(act_back, 1)

            def exp_and_ln_tables():
                nc.scalar.add_instruction(mybir.InstLoadActFuncSet(
                    act_func_set_id=6, name=nc.get_next_instruction_name(), engine=nc.scalar.engine, ins=[], outs=[]))

            def front_xd(d, f):
                after(act, "pe_front", f"xd{d}", f)
                if not (isinstance(f, int) and f < 1):
                    wait(act, bc_out, f * 32)
                act_fn(XD[:, d, :], GF[0:RANK + 2 * NS, :], ACT.Copy).then_inc(act_front, 1)

            def front_dt(q, f):
                after(act, "pe_front", f"dt{q}", f)
                if not (isinstance(f, int) and f < 1):
                    wait(act, dd_out[q], f * 32)
                act_fn(SPA[:, q, :], GF[:, :], ACT.Identity, bias=db[:, q:q + 1]).then_inc(act_front, 1)

            def front_soft(n, q, f):
                if n == "abs":
                    after(act, "act_front", f"dt{q}", f)
                    act_fn(SPB[:, q, :], SPA[:, q, :], ACT.Abs).then_inc(act_front, 1)
                if n == "exp":
                    after(act, "act_front", f"abs{q}", f)
                    act_fn(SPB[:, q, :], SPB[:, q, :], ACT.Exp, scale=-1.0).then_inc(act_front, 1)
                if n == "square":
                    after(act, "act_front", f"exp{q}", f)
                    act.wait_ge(bc_out, 32 * (f + 1))
                    act_fn(FG[:, q, :], SPB[:, q, :], ACT.Square, scale=3.0 ** -0.5,
                           bias=root[:, 0:1]).then_inc(act_front, 1)

            def front_ln(q, f):
                after(act, "dve_front", f"large{q}", f)
                act_fn(SPB[:, q, :], SPB[:, q, :], ACT.Ln, bias=1.0).then_inc(act_front, 1)

            def back_xT(b):
                after(act, "pe_back", "xT", b)
                act_fn(X2T[:, :], GB[1][:, :], ACT.Copy).then_inc(act_back, 1)

            def back_a(m, b):
                after(act, "pe_back", f"a{m}", b)
                act_fn(FA[:, m, :], GB[m % 2][:, :], ACT.Copy, scale=s1c[:, m:m + 1]).then_inc(act_back, 1)

            def back_h(n, m, b):
                dst, col = ((FG, h1c), (FA, h2c))[n - 1]
                if n == 1 and m == 0 and not (isinstance(b, int) and b > G - 3):
                    after(act, "dve_front", f"delta{NQ - 1}", b + 2)
                after(act, "pe_back", f"h{n}_{m}", b)
                act_fn(dst[:, m, :], GB[m % 2][:, :], ACT.Copy, scale=col[:, m:m + 1]).then_inc(act_back, 1)

            def gelu(n, m, b):
                buf = (FG, FA)[n - 1]
                after(act, "act_back", f"h{n}_{m}", b)
                act_fn(buf[:, m, :], buf[:, m, :], ACT.Gelu).then_inc(act_back, 1)

            def iteration(g, par, front, back):
                f, b, fp = g + 1, g - 1, 1 - par
                for p in range(UNITS):
                    d, dt, k, r = unit(p)
                    slot = (p // UQ) % 2
                    first = 0 if d == 0 else L - 1
                    lo, hi = (1, L) if d == 0 else (0, L - 1)
                    wait(act, scan_done, g * UNITS + p - 1)
                    if p % (2 * UQ) < 2:
                        act_fn(dA[p % 2][:, :, first], zero2[:, :], ACT.Copy).then_inc(zero_set, 1)
                    if p % UQ == 0:
                        act.wait_ge(rep_in[slot], 64 * (2 * g + p // UQ // 2 + 1))
                    act_fn(dA[p % 2][:, :, lo:hi],
                           REP[:, slot, r, :].rearrange("p (s l) -> p s l", s=SPG)[:, :, lo:hi],
                           ACT.Exp, scale=AR[:, 8 * d + NR * dt + r, k:k + 1]).then_inc(dA_ready, 1)
                    if front:
                        for _ in at("act_xT", p):
                            front_xT(f, fp)
                        for q in at("act_conv", p):
                            front_conv(q, f, fp)
                        for q in at("act_xd", p):
                            front_xd(q, f)
                        for q in at("act_dt", p):
                            front_dt(q, f)
                        for s_ in at("act_soft", p):
                            for n, q in SOFT:
                                if ("abs", "exp", "square").index(n) + q == s_:
                                    front_soft(n, q, f)
                        for q in at("act_z", p):
                            front_z(q, f, fp)
                    if back:
                        for _ in at("act_bxT", p):
                            back_xT(b)
                        for m in at("act_a", p):
                            back_a(m, b)
                        for m in at("act_h1", p):
                            back_h(1, m, b)
                        for m in at("act_h2", p):
                            back_h(2, m, b)
                    if front:
                        for q in at("act_silu_u", p):
                            silu_u(q, f, fp)
                        for q in at("act_silu_z", p):
                            silu_z(q, f, fp)
                    if back:
                        for m in at("act_silu_a", p):
                            silu_a(m, b)
                        for n in (1, 2):
                            for m in at(f"act_gelu{n}", p):
                                gelu(n, m, b)
                    if any(p in AT[n] for n in (["act_silu_u", "act_silu_z"] if front else [])
                           + (["act_silu_a", "act_gelu1", "act_gelu2"] if back else [])):
                        exp_and_ln_tables()
                    if front:
                        for q in at("act_ln", p):
                            front_ln(q, f)

            exp_and_ln_tables()
            act.wait_ge(const_ok, 2)
            act.wait_ge(w_conv, 16 * N_CONV)
            front_xT(0, 0)
            for q in range(NQ):
                front_conv(q, 0, 0)
            act.wait_ge(w_front, 16 * N_FRONT)
            act_fn(AR[:, :, :], AR[:, :, :], ACT.Exp).then_inc(a_exp, 1)
            for q in range(NQ):
                silu_u(q, 0, 0)
            for d in range(2):
                front_xd(d, 0)
            exp_and_ln_tables()
            for q in range(NQ):
                front_dt(q, 0)
            for n, q in SOFT:
                front_soft(n, q, 0)
            for q in range(NQ):
                front_z(q, 0, 0)
            for q in range(NQ):
                silu_z(q, 0, 0)
            exp_and_ln_tables()
            for q in range(NQ):
                front_ln(q, 0)
            act.wait_ge(we_pe, 1)
            act_fn(WE[:, :, :], GB[0][:, :].rearrange("p (q c) -> p q c", c=C), ACT.Copy).then_inc(we_act, 1)
            act.wait_ge(dprep, DVE_SETUP.index("a_rep") + 1)
            iteration(0, 0, True, False)
            with act.Fori(0, G // 2 - 1) as i:
                iteration(2 * i + 1, 1, True, True)
                iteration(2 * i + 2, 0, True, True)
            iteration(G - 1, 1, False, True)
            after(act, "pe_tail", "xT", 0)
            act_fn(X2T[:, :], SET2[2], ACT.Copy).then_inc(act_tail, 1)
            for m in range(HT):
                after(act, "pe_tail", f"a{m}", 0)
                act_fn(FA[:, m, :], SET1[m], ACT.Silu, scale=s1c[:, m:m + 1]).then_inc(act_tail, 1)
            for n, dst, col, banks in ((1, FG, h1c, SET1), (2, FA, h2c, SET2)):
                for m in range(HT):
                    after(act, "pe_tail", f"h{n}_{m}", 0)
                    act_fn(dst[:, m, :], banks[m], ACT.Gelu, scale=col[:, m:m + 1]).then_inc(act_tail, 1)

        @block.vector
        def _(dve):
            def done(table, step, g):
                after(dve, table, step, g)

            def stats(src, st, s_):
                for t in range(NT):
                    i_ = nc.vector.bn_stats(st[:, t, :], src[:, t, :])
                i_.then_inc(s_, 1)

            def aggregate(n, st, mv, rs, stage, s_, g):
                for t in range(NT):
                    i_ = nc.vector.bn_aggr(mv[:, t, :], st[:, t, :])
                i_.then_inc(s_, 1)
                done(stage, "aggr" + n, g)
                nc.vector.tensor_scalar(rs[:, 0, :], mv[:, :, 1], EPS, None, ALU.add).then_inc(s_, 1)

            def normalise(dst, src, mv, rs, s_):
                for t in range(NT):
                    i_ = nc.vector.tensor_scalar(dst[:, t, :], src[:, t, :], mv[:, t, 0:1], rs[:, 1, t:t + 1],
                                                 ALU.subtract, ALU.mult)
                i_.then_inc(s_, 1)

            def front_moments(f):
                dve.wait_ge(x_in, 16 * (f + 1))
                stats(XT, STF, dve_front)

            def front_aggregate(f):
                aggregate("", STF, MVF, RSF, "dve_front", dve_front, f)

            def front_norm(f):
                done("pool_front", "rstd", f)
                normalise(XT, XT, MVF, RSF, dve_front)

            def front_series(q, f):
                done("act_front", f"square{q}", f)
                nc.vector.scalar_tensor_tensor(FG[:, q, :], FG[:, q, :], 13.0 / 16, SPB[:, q, :],
                                               ALU.add, ALU.mult).then_inc(dve_front, 1)
                nc.vector.tensor_scalar(big[:, q, :], SPB[:, q, :], SMALL, None, ALU.is_ge).then_inc(dve_front, 1)

            def front_select_wait(q, f):
                done("dve_front", f"large{q}", f)
                done("act_front", f"ln{q}", f)

            def front_select(q):
                nc.vector.copy_predicated(FG[:, q, :], big[:, q, :], SPB[:, q, :]).then_inc(dve_front, 1)

            def front_delta(q, f):
                done("dve_front", f"select{q}", f)
                nc.vector.scalar_tensor_tensor(SPB[:, q, :], SPA[:, q, :], 0.0, FG[:, q, :],
                                               ALU.max, ALU.add).then_inc(dve_front, 1)

            def tokens(bank):
                return bank.rearrange("p (t c) -> p t c", c=C)

            bank0, tail_in, tail_out = tokens(GB[0][:, :]), tokens(GF[:, :]), tokens(SET1[0])

            def back_moments(n, b, tail=False):
                if n in "ad":
                    step = {"a": "combine", "d": "w3"}[n]
                    done("pe_tail", step, 0) if tail else done("pe_back", step, b)
                if n == "b":
                    done("pool_back", "lnb", b)
                if n == "c":
                    done("pool_back", "res_b", b)
                src = {"a": tail_in if tail else bank0, "b": TA, "c": X1, "d": tail_out if tail else bank0}[n]
                stats(src, STB, dve_back)

            def back_norm(n, b, tail=False):
                done("pool_back", "rstd_" + n, b)
                src = {"a": tail_in if tail else bank0, "b": TA, "c": X1, "d": tail_out if tail else bank0}[n]
                normalise(TA, src, MVB, RSB, dve_back)

            def back_b(m, b, tail=False):
                if tail:
                    done("pe_tail", f"b{m}", 0)
                    done("act_tail", f"a{m}", 0)
                else:
                    done("pe_back", f"b{m}", b)
                    done("act_back", f"silu{m}", b)
                nc.vector.scalar_tensor_tensor(FA[:, m, :], SET2[m] if tail else GB[m % 2][:, :], s2c[:, m:m + 1],
                                               FA[:, m, :], ALU.mult, ALU.mult).then_inc(dve_back, 1)

            def back_aggregate(n, b):
                aggregate("_" + n, STB, MVB, RSB, "dve_back", dve_back, b)

            def gate(q, g, par):
                wait(dve, y_ready, NQ * g + q + 1)
                nc.vector.tensor_tensor(SZ[:, par, q, :], Y[:, :], SZ[:, par, q, :], ALU.mult).then_inc(gated, 1)

            def scan(p, g):
                d = unit(p)[0]
                wait(dve, dA_ready, g * UNITS + p + 1)
                wait(dve, dbu_ready, g * UNITS + p + 1)
                wait(dve, prod_ready, g * UNITS + p - 1)
                a_, b_, h_ = dA[p % 2][:, :, :].rearrange("p s l -> p (s l)"), DB[:, p % NDB, :], HP[p % 2][:, :]
                if d == 1:
                    a_, b_, h_ = a_[:, ::-1], b_[:, ::-1], h_[:, ::-1]
                nc.vector.tensor_tensor_scan(h_, a_, b_, 0.0, ALU.mult, ALU.add).then_inc(scan_done, 1)

            def product(p, g):
                d, dt, k, r = unit(p)
                if p % (2 * UQ) == 0:
                    dve.wait_ge(bc_in[d], 64 * (g + 1))
                if p % NR == 0:
                    wait(dve, sums_done, UNITS // NR * g + p // NR - 1)
                wait(dve, scan_done, g * UNITS + p + 1)
                nc.vector.tensor_tensor(PR[:, (p // NR) % 2, r, :], HP[p % 2][:, :], BC[:, d, NK + k, :],
                                        ALU.mult).then_inc(prod_ready, 1)

            def iteration(g, par, front, back):
                f, b, fp = g + 1, g - 1, 1 - par
                for p in range(UNITS):
                    if front:
                        for _ in at("dve_stats", p - 1):
                            done("dve_front", "stats", f)
                        for q in at("dve_select", p):
                            front_select_wait(q, f)
                    if back:
                        for n in "abcd":
                            for _ in at("dve_" + n, p - 1):
                                done("dve_back", "stats_" + n, b)
                    scan(p, g)
                    if p > 0:
                        product(p - 1, g)
                    for q in at("dve_gate", p):
                        gate(q, g, par)
                    if back:
                        for _ in at("dve_last_gate", p):
                            gate(NQ - 1, b, fp)
                        for n in "abcd":
                            for _ in at("dve_" + n, p - 1):
                                back_aggregate(n, b)
                            for _ in at("dve_" + n, p):
                                back_moments(n, b)
                        for n in "abc":
                            for _ in at("dve_norm_" + n, p):
                                back_norm(n, b)
                        for m in at("dve_mul", p):
                            back_b(m, b)
                    if front:
                        for _ in at("dve_stats", p - 1):
                            front_aggregate(f)
                        for _ in at("dve_stats", p):
                            front_moments(f)
                        for _ in at("dve_norm", p):
                            front_norm(f)
                        for q in at("dve_series", p):
                            front_series(q, f)
                        for q in at("dve_select", p):
                            front_select(q)
                            front_delta(q, f)
                product(UNITS - 1, g)
                if back:
                    back_norm("d", b)

            def tap(q):
                o = tapT[:, q // DT, :, 128 * (q % DT):128 * (q % DT + 1)]
                i_ = n_in[:, q // DT, 128 * (q % DT):128 * (q % DT + 1)].rearrange("p (a c) -> p a c", a=1)
                nc.vector.tensor_tensor(o, o, i_.to_broadcast([128, TAPS, 128]), ALU.mult).then_inc(dprep, 1)

            front_moments(0)
            done("dve_front", "stats", 0)
            front_aggregate(0)
            dve.wait_ge(w_conv, 16 * N_CONV)
            tap(0)
            front_norm(0)
            for q in range(1, NQ):
                tap(q)
            dve.wait_ge(const_ok, 2)
            nc.vector.tensor_reduce(fold[:, :], ident[:, :].rearrange("p (j d) -> p d j", d=DW), op=ALU.add,
                                    axis=AX.X).then_inc(dprep, 1)
            for q in range(NQ):
                i_ = nc.vector.tensor_scalar(DD[:, q, :], ident[:, :], dp[:, q:q + 1], None, ALU.mult)
            i_.then_inc(dprep, 1)
            dve.wait_ge(a_exp, 1)
            nc.vector.tensor_scalar(AR[:, :, :], AR[:, :, :], -1.0, None, ALU.mult).then_inc(dprep, 1)
            dve.wait_ge(w_comb, 16 * N_COMB)
            nc.vector.tensor_tensor(P12[:, :], PT[:, 0, :], PT[:, 1, :], ALU.add).then_inc(dprep, 1)
            for q in range(NQ):
                front_series(q, 0)
            for q in range(NQ):
                front_select_wait(q, 0)
                front_select(q)
                front_delta(q, 0)
            dve.wait_ge(w_back, 16 * N_BACK)
            nc.vector.tensor_tensor(w3T[:, :, :], w3T[:, :, :],
                                    w3row.rearrange("p (a c) -> p a c", a=1).to_broadcast([128, HT, C]),
                                    ALU.mult).then_inc(dprep, 1)
            iteration(0, 0, True, False)
            with dve.Fori(0, G // 2 - 1) as i:
                iteration(2 * i + 1, 1, True, True)
                iteration(2 * i + 2, 0, True, True)
            iteration(G - 1, 1, False, True)
            b = G - 1
            gate(NQ - 1, b, 1)
            for n in "abc":
                back_moments(n, b, tail=True)
                done("dve_back", "stats_" + n, b)
                back_aggregate(n, b)
                back_norm(n, b, tail=True)
            for m in range(HT):
                back_b(m, b, tail=True)
            back_moments("d", b, tail=True)
            done("dve_back", "stats_d", b)
            back_aggregate("d", b)
            back_norm("d", b, tail=True)

        @block.tensor
        def _(pe):
            mm = nc.tensor.matmul

            def done(table, step, g):
                after(pe, table, step, g)

            def front_bank(step, f):
                steps = [s_ for s_ in ACT_FRONT if s_ in PE_FRONT]
                at = steps.index(step)
                done("act_front", steps[at - 1], f) if at else done("act_front", steps[-1], f - 1)

            def front_xT(f):
                front_bank("xT", f)
                done("dve_front", "norm", f)
                for t in range(NT):
                    i_ = nc.tensor.transpose(GF[:, 128 * t:128 * (t + 1)], XT[:, t, :], ident[:, :])
                i_.then_inc(pe_front, 1)

            def front_conv(q, f, par):
                d, t = q // DT, q % DT
                front_bank(f"conv{q}", f)
                for k in range(TAPS):
                    at = k if d == 0 else 2 * PAD - k
                    i_ = mm(GF[:, :], tapT[:, d, k, 128 * t:128 * (t + 1)], XNT[:, par, :, at:at + L],
                            start=(k == 0), stop=(k == TAPS - 1))
                i_.then_inc(pe_front, 1)

            def front_z(q, f, par):
                front_bank(f"z{q}", f)
                mm(GF[:, :], zT[:, q, :], XNT[:, par, :, PAD:PAD + L], start=True, stop=True).then_inc(pe_front, 1)

            def front_xd(d, f, par):
                if d == 0:
                    done("act_front", f"silu_u{NQ - 1}", f)
                front_bank(f"xd{d}", f)
                for t in range(DT):
                    i_ = mm(GF[0:RANK + 2 * NS, :], xpT[:, d * DT + t, :], U[:, par, d * DT + t, :],
                            start=(t == 0), stop=(t == DT - 1))
                i_.then_inc(pe_front, 1)

            def front_dt(q, f):
                front_bank(f"dt{q}", f)
                mm(GF[:, :], dtT[:, q, :], XD[0:RANK, q // DT, :], start=True, stop=True).then_inc(pe_front, 1)

            def combine(b, par):
                wait(pe, gated, NQ * (b + 1))
                after(pe, "dve_back", "norm_d", b - 1)
                for t in range(NT):
                    o = GB[0][:, C * t:C * (t + 1)]
                    tok = slice(128 * t, 128 * (t + 1))
                    for q in range(NQ):
                        mm(o, SZ[:, par, q, tok], WE[:, q, :], start=(q == 0), stop=False)
                    s_, h_ = t * 128 // L, t * 128 % L
                    mm(o, XNT[:, par, s_, PAD + h_:PAD + h_ + 128], P12[:, :], start=False, stop=False)
                    i_ = mm(o, ones[:, :], pbrow[:, :], start=False, stop=True)
                i_.then_inc(pe_back, 1)

            def back_xT(b):
                done("dve_back", "norm_c", b)
                for t in range(NT):
                    i_ = nc.tensor.transpose(GB[1][:, 128 * t:128 * (t + 1)], TA[:, t, :], ident[:, :])
                i_.then_inc(pe_back, 1)

            def back_up(n, m, b):
                w_ = {"a": w1T, "b": w2T}[n]
                if n == "a":
                    done("act_back", "xT", b)
                    done("dve_back", "norm_a", b) if m == 0 else None
                    done("act_back", f"a{m - 2}", b) if m >= 2 else None
                else:
                    done("act_back", f"a{m + 2}", b) if m < 2 else done("dve_back", f"b{m - 2}", b)
                mm(GB[m % 2][:, :], w_[:, 128 * m:128 * (m + 1)], X2T[:, :], start=True, stop=True).then_inc(pe_back, 1)

            def back_h(n, m, b):
                w_, src = ((h1T, FA), (h2T, FG))[n - 1]
                if n == 1:
                    done("dve_back", f"b{HT - 1}", b)
                elif m == 0:
                    done("act_back", f"h1_{HT - 1}", b)
                if m >= 2:
                    done("act_back", f"h{n}_{m - 2}", b)
                for k in range(HT):
                    if n == 2 and m == 0:
                        done("act_back", f"gelu1_{k}", b)
                    i_ = mm(GB[m % 2][:, :], w_[:, k, 128 * m:128 * (m + 1)], src[:, k, :],
                            start=(k == 0), stop=(k == HT - 1))
                i_.then_inc(pe_back, 1)

            def back_w3(b):
                done("act_back", f"gelu2_{HT - 1}", b)
                for t in range(NT):
                    for k in range(HT):
                        i_ = mm(GB[0][:, C * t:C * (t + 1)], FA[:, k, 128 * t:128 * (t + 1)], w3T[:, k, :],
                                start=(k == 0), stop=(k == HT - 1))
                i_.then_inc(pe_back, 1)

            def sums(s_, g, par):
                q = s_ * NR // UQ
                last = s_ % NK == NK - 1
                if s_ % NK == 0:
                    wait(pe, gated, NQ * g + q)
                    mm(Y[:, :], DD[:, q, :], U[:, par, q, :], start=True, stop=False)
                wait(pe, prod_ready, g * UNITS + NR * (s_ + 1))
                for r in range(NR):
                    i_ = mm(Y[DW * r:DW * (r + 1), :], fold[:, :], PR[:, s_ % 2, r, :], start=False, stop=last)
                i_.then_inc(sums_done, 1)
                if last:
                    pe.wait_ge(sums_done, UNITS // NR * g + s_ + 1)
                    pe.sem_inc(y_ready, 1)

            def iteration(g, par, front, back):
                f, b, fp = g + 1, g - 1, 1 - par
                late = AT["pe_sums"][0]
                for p in range(UNITS):
                    if p % NR == late and p > NR:
                        sums(p // NR - 1, g, par)
                    if back:
                        for _ in at("pe_combine", p):
                            combine(b, fp)
                        for _ in at("pe_bxT", p):
                            back_xT(b)
                        for m in at("pe_a", p):
                            back_up("a", m, b)
                        for m in at("pe_b", p):
                            back_up("b", m, b)
                        for n in (1, 2):
                            for m in at(f"pe_h{n}", p):
                                back_h(n, m, b)
                        for _ in at("pe_w3", p):
                            back_w3(b)
                    if front:
                        for _ in at("pe_xT", p):
                            front_xT(f)
                        for q in at("pe_conv", p):
                            front_conv(q, f, fp)
                        for d in at("pe_xd", p):
                            front_xd(d, f, fp)
                        for q in at("pe_dt", p):
                            front_dt(q, f)
                        for q in at("pe_z", p):
                            front_z(q, f, fp)
                    if g is last_group and p == UNITS - 3:
                        tail_combine(False)
                sums(UNITS // NR - 1, g, par)

            last_group = G - 1

            def tail_combine(end):
                if not end:
                    wait(pe, gated, NQ * G - 1)
                    done("act_front", ACT_FRONT[-1], G - 1)
                else:
                    wait(pe, gated, NQ * G)
                for t in range(NT):
                    o = GF[:, C * t:C * (t + 1)]
                    tok = slice(128 * t, 128 * (t + 1))
                    if end:
                        i_ = mm(o, SZ[:, 1, NQ - 1, tok], WE[:, NQ - 1, :], start=False, stop=(t == NT - 1))
                    else:
                        for q in range(NQ - 1):
                            mm(o, SZ[:, 1, q, tok], WE[:, q, :], start=(t == 0 and q == 0), stop=False)
                        s_, h_ = t * 128 // L, t * 128 % L
                        mm(o, XNT[:, 1, s_, PAD + h_:PAD + h_ + 128], P12[:, :], start=False, stop=False)
                        mm(o, ones[:, :], pbrow[:, :], start=False, stop=False)
                if end:
                    i_.then_inc(pe_tail, 1)

            pe.wait_ge(const_ok, 2)
            front_xT(0)
            for q in range(NQ):
                pe.wait_ge(dprep, DVE_SETUP.index(f"tap{q}") + 1)
                front_conv(q, 0, 0)
            pe.wait_ge(w_front, 16 * N_FRONT)
            for d in range(2):
                front_xd(d, 0, 0)
            for q in range(NQ):
                front_dt(q, 0)
            for q in range(NQ):
                front_z(q, 0, 0)
            pe.wait_ge(w_comb, 16 * N_COMB)
            for q in range(NQ):
                i_ = mm(GB[0][:, C * q:C * (q + 1)], n_out[:, q, :], PT[:, q // DT, :], start=True, stop=True)
            i_.then_inc(we_pe, 1)
            pe.wait_ge(we_act, 1)
            pe.wait_ge(dprep, len(DVE_SETUP))
            pe.wait_ge(w_back, 16 * N_BACK)
            iteration(0, 0, True, False)
            with pe.Fori(0, G // 2 - 1) as i:
                iteration(2 * i + 1, 1, True, True)
                iteration(2 * i + 2, 0, True, True)
            iteration(G - 1, 1, False, True)
            b = G - 1
            tail_combine(True)
            done("dve_back", "norm_c", b)
            done("act_back", f"h2_{HT - 1}", b - 1)
            for t in range(NT):
                i_ = nc.tensor.transpose(SET2[2][:, 128 * t:128 * (t + 1)], TA[:, t, :], ident[:, :])
            i_.then_inc(pe_tail, 1)
            wait(pe, scan_done, UNITS * G)
            wait(pe, prod_ready, UNITS * G)
            done("act_tail", "xT", 0)
            for w_, banks in ((w1T, SET1), (w2T, SET2)):
                for m in range(HT):
                    mm(banks[m], w_[:, 128 * m:128 * (m + 1)], X2T[:, :], start=True, stop=True).then_inc(pe_tail, 1)
            for n, w_, src, banks in ((1, h1T, FA, SET1), (2, h2T, FG, SET2)):
                for k in range(HT):
                    done("dve_back", f"b{k}", b) if n == 1 else done("act_tail", f"h1_{k}", 0)
                    for m in range(HT):
                        if n == 1 and k == 0:
                            done("act_tail", f"a{m}", 0)
                        i_ = mm(banks[m], w_[:, k, 128 * m:128 * (m + 1)], src[:, k, :],
                                start=(k == 0), stop=(k == HT - 1))
                        if k == HT - 1:
                            i_.then_inc(pe_tail, 1)
            for k in range(HT):
                done("act_tail", f"h2_{k}", 0)
                for t in range(NT):
                    i_ = mm(SET1[0][:, C * t:C * (t + 1)], FA[:, k, 128 * t:128 * (t + 1)], w3T[:, k, :],
                            start=(t == 0 and k == 0), stop=(t == NT - 1 and k == HT - 1))
            i_.then_inc(pe_tail, 1)


def kernel(L0_attn_x, L0_attn_proj_w, L0_attn_proj_b, L0_attn_ln_w, L0_attn_ln_b, **rest):
    import numpy as _np
    import concourse.bacc as _bacc
    from concourse import mybir as _mybir
    from concourse.bass_utils import run_bass_kernel_spmd as _run

    def both(name):
        return _np.stack([_np.asarray(rest[f"L0_attn_{d}_{name}"]) for d in ("fw", "bw")])

    def ffn(name):
        return _np.asarray(rest[f"L0_ffn_{name}"])

    def columns(v):
        return v.reshape(-1, 128).T

    def rows_on_partitions(w_t):
        return w_t.reshape(-1, 128, w_t.shape[-1]).transpose(1, 0, 2)

    laid = {
        "x": _np.asarray(L0_attn_x),
        "in_t": both("in_w").transpose(2, 0, 1),
        "taps": both("conv_w")[:, :, 0, :].transpose(0, 2, 1).reshape(1, -1),
        "xproj_t": rows_on_partitions(both("xproj_w").transpose(0, 2, 1).reshape(2 * DI, -1)),
        "dt_t": both("dt_w").transpose(2, 0, 1).reshape(RANK, NQ, 128),
        "a_log": both("Alog").reshape(2, DI // DW, DW, NK, NJ).transpose(4, 2, 0, 1, 3).reshape(128, -1, NK),
        "columns": _np.concatenate([columns(v) for v in (both("conv_b"), both("dt_b"), both("Dp"), ffn("w1_s"),
                                                         ffn("w2_s"), ffn("h1_s"), ffn("h2_s"))], axis=1),
        "out_w": both("out_w").transpose(1, 0, 2).reshape(128, NQ, 128),
        "proj_t": _np.asarray(L0_attn_proj_w).T.reshape(2, C, C).transpose(1, 0, 2),
        "proj_b": _np.asarray(L0_attn_proj_b).reshape(1, C),
        "ln_w": _np.asarray(L0_attn_ln_w).reshape(1, C),
        "ln_b": _np.asarray(L0_attn_ln_b).reshape(1, C),
        "w1_t": ffn("w1_w").T, "w2_t": ffn("w2_w").T,
        "h1_t": rows_on_partitions(ffn("h1_w").T), "h2_t": rows_on_partitions(ffn("h2_w").T),
        "w3_t": rows_on_partitions(ffn("w3_w").T), "w3_s": ffn("w3_s").reshape(1, C),
    }
    nc = _bacc.Bacc("TRN2", target_bir_lowering=False, num_devices=1)
    arrays, args = {}, {}
    for name, a in laid.items():
        a = _np.ascontiguousarray(a)
        arrays[f"in_{name}_dram"] = a
        args[name] = nc.dram_tensor(f"in_{name}_dram", a.shape, _mybir.dt.from_np(a.dtype), kind="ExternalInput").ap()
    out = nc.dram_tensor("out_0_dram", (SEQS, L, C), _mybir.dt.float32, kind="ExternalOutput").ap()
    build(nc, args.pop("x"), args, out)
    r = _run(nc, [arrays], core_ids=[0])
    return r.results[0]["out_0_dram"]
```

```python
import concourse.bass as bass
from concourse import mybir
from contextlib import ExitStack

SEQS, L, C = 16, 256, 128
DI, NS, RANK, TAPS = 256, 16, 8, 4
HID = 512
SPG = 2
T = SPG * L
G = SEQS // SPG
NT = T // 128
DT = DI // 128
NQ = 2 * DT
NJ, DW = 4, 32
NK = NS // NJ
NR = 128 // DW
UNITS = NQ * NK * NR
UQ = NK * NR
PAD = TAPS - 1
LP = L + 2 * PAD
HT = HID // 128
EPS = 1e-5
SMALL = 2.0 ** -7
NDB = 4

SOFT = [(n, s - i) for s in range(NQ + 2) for i, n in enumerate(("abs", "exp", "square")) if 0 <= s - i < NQ]
SOFT_STEPS = NQ + 2


def each(name, n):
    return [f"{name}{i}" for i in range(n)]


PE_FRONT = ["xT"] + each("conv", NQ) + each("xd", 2) + each("dt", NQ) + each("z", NQ)
ACT_FRONT = ["xT"] + each("conv", NQ) + each("silu_u", NQ) + each("xd", 2) + each("dt", NQ) \
    + [f"{n}{q}" for n, q in SOFT] + each("ln", NQ) + each("z", NQ) + each("silu_z", NQ)
DVE_FRONT = ["stats", "aggr", "var", "norm"] + [f"{n}{q}" for q in range(NQ) for n in ("series", "large")] \
    + [f"{n}{q}" for q in range(NQ) for n in ("select", "delta")]
POOL_FRONT = ["rstd"] + each("du", NQ)
PE_BACK = ["combine", "xT"] + each("a", HT) + each("b", HT) + each("h1_", HT) + each("h2_", HT) + ["w3"]
ACT_BACK = ["xT"] + each("a", HT) + each("silu", HT) + each("h1_", HT) + each("gelu1_", HT) \
    + each("h2_", HT) + each("gelu2_", HT)
DVE_BACK = ["stats_a", "aggr_a", "var_a", "norm_a", "stats_b", "aggr_b", "var_b", "norm_b",
            "stats_c", "aggr_c", "var_c", "norm_c"] + each("b", HT) + ["stats_d", "aggr_d", "var_d", "norm_d"]
POOL_BACK = ["rstd_a", "lnw", "lnb", "rstd_b", "res_b", "rstd_c", "rstd_d", "res_d"]
HALVES = ((0, 1), (2, 3))
PE_FIRST = ["xT", "conv0", "conv1", "xd0", "dt0", "dt1", "conv2", "conv3"] + each("z", NQ) + ["xd1", "dt2", "dt3"]
ACT_FIRST = ["xT", "silu_u0", "silu_u1", "xd0", "dt0", "dt1"] \
    + [f"{n}{q}" for n in ("abs", "exp", "square", "ln") for q in HALVES[0]] \
    + ["silu_u2", "silu_u3"] + each("silu_z", NQ) + ["xd1", "dt2", "dt3"] \
    + [f"{n}{q}" for n in ("abs", "exp", "square", "ln") for q in HALVES[1]]
DVE_FIRST = ["stats", "aggr", "var", "norm"] + [f"{n}{q}" for h in HALVES for two in (("series", "large"), ("select", "delta"))
                                                for q in h for n in two]
FIRST_READ_BY = {"conv": "silu_u", "z": "silu_z"}
FRONT_BANKS = {"conv1": "back1", "conv3": "back1", "xd1": "back0", "dt1": "back0", "dt3": "back0"}
FIRST_BANKS = FRONT_BANKS | {"z1": "back1", "z3": "back1"}
PE_TAIL = PE_BACK
ACT_TAIL = ["xT"] + each("a", HT) + each("h1_", HT) + each("h2_", HT)

AT = {
    "pe_combine": [1], "pe_xT": [5], "pe_conv": [9, 11, 13, 15], "pe_xd": [18, 19], "pe_dt": [20, 20, 22, 23],
    "pe_z": [31, 32, 33, 34], "pe_bxT": [22], "pe_a": [24, 25, 26, 27], "pe_b": [28, 29, 30, 31],
    "pe_h1": [36, 38, 40, 42], "pe_h2": [45, 47, 49, 51], "pe_w3": [58], "act_xT": [8],
    "act_conv": [11, 13, 16, 17], "act_silu_u": [17, 17, 17, 17], "act_xd": [19, 19], "act_dt": [21, 22, 23, 24],
    "act_soft": [24, 24, 25, 26, 27, 28], "act_z": [33, 33, 34, 34], "act_silu_z": [35, 35, 35, 35],
    "act_ln": [30, 31, 32, 33], "act_bxT": [22], "act_a": [28, 29, 30, 31], "act_silu_a": [31, 31, 31, 31],
    "act_h1": [39, 41, 43, 45], "act_gelu1": [45, 45, 45, 45], "act_h2": [48, 50, 52, 55],
    "act_gelu2": [55, 55, 55, 55], "pool_rstd": [6], "pool_a": [12], "pool_ln": [14, 15], "pool_b": [17],
    "pool_res_b": [17], "pool_c": [20], "pool_d": [61], "pool_du": [36, 37, 38, 39], "dve_stats": [1],
    "dve_norm": [6], "dve_gate": [17, 33, 49], "dve_last_gate": [0], "dve_series": [27, 28, 29, 29],
    "dve_select": [32, 33, 34, 35], "dve_a": [7], "dve_norm_a": [11], "dve_b": [14], "dve_norm_b": [15],
    "dve_c": [16], "dve_norm_c": [18], "dve_mul": [30, 31, 32, 33], "dve_d": [57], "pe_sums": [1],
}


def at(name, p):
    return [i for i, unit_ in enumerate(AT[name]) if unit_ == p]


def build(nc, x, w, out):
    f32 = mybir.dt.float32
    ALU, ACT, AX = mybir.AluOpType, mybir.ActivationFunctionType, mybir.AxisListType

    dd = nc.dram_tensor("delta_and_du", (2, NQ, 2, 128, T), f32).ap()
    bc = nc.dram_tensor("b_and_c", (2, 2, 2 * NS, T), f32).ap()
    x_g = x.rearrange("(g s) (h p) c -> g p (s h) c", s=SPG, p=128)
    out_g = out.rearrange("(g s) (h p) c -> g p (s h) c", s=SPG, p=128)

    with ExitStack() as ctx:
        def sb(name, shape):
            return ctx.enter_context(nc.sbuf_tensor(name, shape, f32))

        def pb(name, shape=(128, T)):
            return ctx.enter_context(nc.psum_tensor(name, list(shape), f32))

        def sem(name):
            return ctx.enter_context(nc.semaphore(name))

        REP = sb("rep", [128, 2, 2 * NR, T])
        BC = sb("bc_rep", [128, 2, 2 * NK, T])
        DB = sb("dbu", [128, NDB, T])
        PR = sb("prod", [128, 2, NR, T])
        AR = sb("a_rep", [128, 2 * 8, NK])
        XT = sb("x_tok", [128, NT, C])
        XNT = sb("xn_t", [128, 2, SPG, LP])
        U = sb("u", [128, 2, NQ, T])
        SZ = sb("silu_z", [128, 2, NQ, T])
        SPA = sb("dt_raw", [128, NQ, T])
        SPB = sb("delta", [128, NQ, T])
        TA = sb("normed", [128, NT, C])
        X1 = sb("x1", [128, NT, C])
        X2T = sb("x2_t", [128, T])
        XRES = X2T[:, :].rearrange("p (t c) -> p t c", c=C)
        FA = sb("ffn_a", [128, HT, T])
        FG = sb("ffn_g", [128, HT, T])
        XD = FG[0:RANK + 2 * NS, 0:2, :]
        XD_FIRST = FG[0:RANK + 2 * NS, 2:4, :]
        STF, MVF, RSF = sb("stf", [128, NT, 6]), sb("mvf", [128, NT, 2]), sb("rsf", [128, 2, NT])
        STB, MVB, RSB = sb("stb", [128, NT, 6]), sb("mvb", [128, NT, 2]), sb("rsb", [128, 2, NT])
        ident = sb("ident", [128, 128])
        fold = sb("fold", [128, DW])
        mhalf = sb("minus_half", [128, NT])
        zero2 = sb("zero2", [128, SPG])
        ones = sb("ones", [1, 128])
        pbrow = sb("proj_b_row", [1, C])
        lnw, lnb = sb("lnw", [128, C]), sb("lnb", [128, C])
        tapT = sb("tap_t", [128, 2, TAPS, DI])
        zT = sb("z_t", [128, NQ, 128])
        xpT = sb("xproj_t", [128, NQ, RANK + 2 * NS])
        dtT = sb("dt_t", [RANK, NQ, 128])
        P12 = sb("proj_sum_t", [128, 128])
        WE = sb("w_eff", [128, NQ, C])
        DD = sb("d_diag", [128, NQ, 128])
        w1T, w2T = sb("w1_t", [128, HID]), sb("w2_t", [128, HID])
        h1T, h2T = sb("h1_t", [128, HT, HID]), sb("h2_t", [128, HT, HID])
        w3T = sb("w3_t", [128, HT, C])
        cols = sb("columns", [128, 3 * NQ + 4 * HT])
        cb, db, dp = (cols[:, NQ * i:NQ * (i + 1)] for i in range(3))
        s1c, s2c, h1c, h2c = (cols[:, 3 * NQ + HT * i:3 * NQ + HT * (i + 1)] for i in range(4))
        root = sb("minus_root", [128, 1])
        big = TA[:, :, :].rearrange("p t c -> p (t c)").bitcast(mybir.dt.uint8) \
            .rearrange("p (q l) -> p q l", q=NQ)
        n_in = REP[:, 1, 0, :].rearrange("p (d c) -> p d c", d=2)
        n_out = REP[:, 1, 1, :].rearrange("p (q c) -> p q c", c=128)
        PT = REP[:, 1, 2, 0:2 * C].rearrange("p (d c) -> p d c", d=2)
        w3row = REP[:, 1, 3, 0:C]

        dA = [pb(f"dA{i}", (128, SPG, L)) for i in range(2)]
        HP = [pb(f"h{i}") for i in range(2)]
        Y = pb("y")
        GF = pb("front_bank")
        GB = [pb(f"back_bank{i}") for i in range(2)]
        BANK = {"front": GF, "back0": GB[0], "back1": GB[1]}

        def front_psum(step, f=None):
            return BANK[(FIRST_BANKS if isinstance(f, int) and f == 0 else FRONT_BANKS).get(step, "front")]

        w_conv = sem("w_conv")
        w_front = sem("w_front")
        w_comb = sem("w_comb")
        w_back = sem("w_back")
        const_ok = sem("const_ok")
        dprep = sem("dprep")
        we_pe, we_act = sem("we_pe"), sem("we_act")
        a_exp = sem("a_exp")
        dA_ready, dbu_ready = sem("dA_ready"), sem("dbu_ready")
        scan_done, prod_ready = sem("scan_done"), sem("prod_ready")
        zero_set = sem("zero_set")
        sums_done = sem("sums_done")
        y_ready, gated = sem("y_ready"), sem("gated")
        rep_in = [sem("rep_in0"), sem("rep_in1")]
        bc_in = [sem("bc_in0"), sem("bc_in1")]
        x_in, xres_in, out_done = sem("x_in"), sem("xres_in"), sem("out_done")
        bc_out, dd_out = sem("bc_out"), [sem(f"dd_out{q}") for q in range(NQ)]
        pe_front, act_front, dve_front, pool_front = (sem(n) for n in ("pe_front", "act_front", "dve_front", "pool_front"))
        pe_back, act_back, dve_back, pool_back = (sem(n) for n in ("pe_back", "act_back", "dve_back", "pool_back"))

        pe_tail, act_tail = sem("pe_tail"), sem("act_tail")
        pe_first, act_first, dve_first, pool_first = (sem(n) for n in ("pe_first", "act_first", "dve_first", "pool_first"))

        TABLES = {"pe_front": (pe_front, PE_FRONT), "act_front": (act_front, ACT_FRONT),
                  "dve_front": (dve_front, DVE_FRONT), "pool_front": (pool_front, POOL_FRONT),
                  "pe_back": (pe_back, PE_BACK), "act_back": (act_back, ACT_BACK),
                  "dve_back": (dve_back, DVE_BACK), "pool_back": (pool_back, POOL_BACK),
                  "pe_first": (pe_first, PE_FIRST), "act_first": (act_first, ACT_FIRST),
                  "dve_first": (dve_first, DVE_FIRST), "pool_first": (pool_first, POOL_FRONT),
                  "pe_tail": (pe_tail, PE_TAIL), "act_tail": (act_tail, ACT_TAIL)}

        def wait(eng, s, value):
            if not isinstance(value, int) or value > 0:
                eng.wait_ge(s, value)

        def after(eng, table, step, g):
            if isinstance(g, int) and g < 0:
                return
            if isinstance(g, int) and g == 0:
                table = table.replace("_front", "_first")
                if table == "act_first" and step[:-1] in FIRST_READ_BY:
                    step = FIRST_READ_BY[step[:-1]] + step[-1]
            s, steps = TABLES[table]
            wait(eng, s, g * len(steps) + steps.index(step) + 1)

        def front_sem(eng, f):
            return TABLES[eng + ("_first" if isinstance(f, int) and f == 0 else "_front")][0]

        def end_first(eng, name):
            s, steps = TABLES[name + "_first"]
            eng.wait_ge(s, len(steps))
            eng.sem_inc(TABLES[name + "_front"][0], len(TABLES[name + "_front"][1]))

        def x_dbl(f):
            return XD_FIRST if isinstance(f, int) and f == 0 else XD

        def unit(p):
            q = p // UQ
            return q // DT, q % DT, (p % UQ) // NR, p % NR

        DVE_SETUP = each("tap", NQ) + ["fold", "d_diag", "a_rep", "p12", "w3"]
        N_CONV, N_FRONT, N_COMB, N_BACK = 3, 4, 2, 9
        SET1 = [dA[0][:, :, :].rearrange("p s l -> p (s l)"), dA[1][:, :, :].rearrange("p s l -> p (s l)"),
                HP[0][:, :], HP[1][:, :]]
        SET2 = [Y[:, :], GB[0][:, :], GB[1][:, :], GF[:, :]]

        block = ctx.enter_context(nc.Block())

        @block.sync
        def _(sp):
            def rep_load(q, g, par, slot):
                for j in range(NJ):
                    sp.dma_start(REP[DW * j:DW * (j + 1), slot, :, :],
                                 dd[par, q].rearrange("t (r p) l -> p (t r) l", p=DW)).then_inc(rep_in[slot], 16)

            def bc_load(d, g, par):
                for j in range(NJ):
                    rows = bc[par, d].rearrange("(m j) l -> j m l", j=NJ)[j:j + 1]
                    sp.dma_start(BC[DW * j:DW * (j + 1), d, :, :],
                                 rows.to_broadcast([DW, 2 * NK, T])).then_inc(bc_in[d], 16)

            def half_free(q, g):
                wait(sp, dA_ready, g * UNITS + UQ * (q + 1))
                wait(sp, dbu_ready, g * UNITS + UQ * (q + 1))

            def bc_free(d, g):
                wait(sp, dbu_ready, g * UNITS + 2 * UQ * (d + 1))
                wait(sp, prod_ready, g * UNITS + 2 * UQ * (d + 1))

            def bc_store_one(d, f, par):
                after(sp, "act_front", f"xd{d}", f)
                sp.dma_start(bc[par, d], x_dbl(f)[RANK:RANK + 2 * NS, d, :]).then_inc(bc_out, 16)

            def bc_store(f, par):
                if not (isinstance(f, int) and f < 2):
                    wait(sp, bc_in[0], (f - 1) * 64)
                    wait(sp, bc_in[1], (f - 1) * 64)
                for d in range(2):
                    bc_store_one(d, f, par)

            def dd_store_one(q, f, par):
                after(sp, "dve_front", f"delta{q}", f)
                sp.dma_start(dd[par, q, 0], SPB[:, q, :]).then_inc(dd_out[q], 16)
                after(sp, "pool_front", f"du{q}", f)
                sp.dma_start(dd[par, q, 1], SPA[:, q, :]).then_inc(dd_out[q], 16)

            def dd_store(f, par):
                if not (isinstance(f, int) and f < 2):
                    wait(sp, rep_in[0], (f - 1) * 128)
                    wait(sp, rep_in[1], (f - 1) * 128)
                for q in range(NQ):
                    dd_store_one(q, f, par)

            def iteration(g, par, front, back):
                f, b = g + 1, g - 1
                fp = 1 - par
                if front:
                    after(sp, "pe_front", "xT", f - 1)
                    sp.dma_start(XT[:, :, :], x_g[f]).then_inc(x_in, 16)
                if back:
                    sp.dma_start(XRES, x_g[b]).then_inc(xres_in, 16)
                half_free(3, g - 1)
                rep_load(1, g, par, 1)
                bc_free(1, g - 1)
                bc_load(1, g, par)
                half_free(0, g)
                rep_load(2, g, par, 0)
                if front:
                    bc_store(f, fp)
                half_free(1, g)
                rep_load(3, g, par, 1)
                if front:
                    bc_free(0, g)
                    wait(sp, bc_out, (f + 1) * 32)
                    bc_load(0, f, fp)
                    dd_store(f, fp)
                    half_free(2, g)
                    for q in range(NQ):
                        wait(sp, dd_out[q], (f + 1) * 32)
                    rep_load(0, f, fp, 0)
                if back:
                    after(sp, "pool_back", "res_d", b)
                    sp.dma_start(out_g[b], X1[:, :, :]).then_inc(out_done, 16)

            def load(dst, name, s_):
                sp.dma_start(dst, w[name]).then_inc(s_, 16)

            def load_row(dst, name, shape, s_):
                sp.dma_start(dst, w[name].to_broadcast(shape)).then_inc(s_, 16)

            sp.dma_start(XT[:, :, :], x_g[0]).then_inc(x_in, 16)
            sp.dma_start(n_in, w["in_t"][:, :, 0:DI]).then_inc(w_conv, 16)
            load_row(tapT[:, :, :, :].rearrange("p d k c -> p (d k c)"), "taps", [128, 2 * TAPS * DI], w_conv)
            load(cols[:, :], "columns", w_conv)
            load(xpT[:, :, :], "xproj_t", w_front)
            load(dtT[:, :, :], "dt_t", w_front)
            sp.dma_start(zT[:, :, :].rearrange("p (d t) c -> p d (t c)", d=2), w["in_t"][:, :, DI:2 * DI]).then_inc(w_front, 16)
            load(AR[:, :, :], "a_log", w_front)
            load(n_out, "out_w", w_comb)
            load(PT, "proj_t", w_comb)
            load(pbrow[:, :], "proj_b", w_back)
            load_row(lnw[:, :], "ln_w", [128, C], w_back)
            load_row(lnb[:, :], "ln_b", [128, C], w_back)
            load_row(w3row, "w3_s", [128, C], w_back)
            for dst, name in ((w3T, "w3_t"), (h1T, "h1_t"), (h2T, "h2_t")):
                load(dst[:, :, :], name, w_back)
            for dst, name in ((w1T, "w1_t"), (w2T, "w2_t")):
                load(dst[:, :], name, w_back)

            sp.sem_inc(out_done, 16)
            bc_store_one(0, 0, 0)
            wait(sp, bc_out, 16)
            bc_load(0, 0, 0)
            for q in HALVES[0]:
                dd_store_one(q, 0, 0)
                if q == 0:
                    wait(sp, dd_out[0], 32)
                    rep_load(0, 0, 0, 0)
            bc_store_one(1, 0, 0)
            for q in HALVES[1]:
                dd_store_one(q, 0, 0)
            wait(sp, bc_out, 32)
            for q in range(1, NQ):
                wait(sp, dd_out[q], 32)
            sp.wait_ge(we_act, 1)
            sp.wait_ge(dprep, len(DVE_SETUP))

            iteration(0, 0, True, False)
            with sp.Fori(0, G // 2 - 1) as i:
                iteration(2 * i + 1, 1, True, True)
                iteration(2 * i + 2, 0, True, True)
            iteration(G - 1, 1, False, True)
            sp.dma_start(XRES, x_g[G - 1]).then_inc(xres_in, 16)
            after(sp, "pool_back", "res_d", G - 1)
            sp.dma_start(out_g[G - 1], X1[:, :, :]).then_inc(out_done, 16)
            sp.wait_ge(out_done, 16 * (G + 1))

        @block.gpsimd
        def _(pool):
            def rstd_front(f):
                after(pool, "dve_front", "var", f)
                nc.gpsimd.tensor_tensor(RSF[:, 1, :], RSF[:, 0, :], mhalf[:, :], ALU.pow).then_inc(front_sem("pool", f), 1)

            def rstd_back(n, b):
                after(pool, "dve_back", "var_" + n, b)
                nc.gpsimd.tensor_tensor(RSB[:, 1, :], RSB[:, 0, :], mhalf[:, :], ALU.pow).then_inc(pool_back, 1)

            def broadcast(v):
                return v[:, :].rearrange("p (a c) -> p a c", a=1).to_broadcast([128, NT, C])

            def times_lnw(b):
                after(pool, "dve_back", "norm_a", b)
                nc.gpsimd.tensor_tensor(TA[:, :, :], TA[:, :, :], broadcast(lnw), ALU.mult).then_inc(pool_back, 1)

            def plus_lnb(b):
                after(pool, "pool_back", "lnw", b)
                nc.gpsimd.tensor_tensor(TA[:, :, :], TA[:, :, :], broadcast(lnb), ALU.add).then_inc(pool_back, 1)

            def residual_b(b):
                after(pool, "dve_back", "norm_b", b)
                pool.wait_ge(xres_in, 16 * (b + 1))
                pool.wait_ge(out_done, 16 * (b + 1))
                nc.gpsimd.tensor_tensor(X1[:, :, :], TA[:, :, :], XRES, ALU.add).then_inc(pool_back, 1)

            def residual_d(b):
                after(pool, "dve_back", "norm_d", b)
                nc.gpsimd.tensor_tensor(X1[:, :, :], TA[:, :, :], X1[:, :, :], ALU.add).then_inc(pool_back, 1)

            def front_du(q, f, par):
                after(pool, "dve_front", f"delta{q}", f)
                nc.gpsimd.tensor_tensor(SPA[:, q, :], SPB[:, q, :], U[:, par, q, :], ALU.mult).then_inc(front_sem("pool", f), 1)

            def iteration(g, par, front, back):
                f, b, fp = g + 1, g - 1, 1 - par
                for p in range(UNITS):
                    d, dt, k, r = unit(p)
                    slot = (p // UQ) % 2
                    if p % UQ == 0:
                        pool.wait_ge(rep_in[slot], 64 * (2 * g + p // UQ // 2 + 1))
                    if p % (2 * UQ) == 0:
                        pool.wait_ge(bc_in[d], 64 * (g + 1))
                    wait(pool, scan_done, g * UNITS + p - NDB + 1)
                    nc.gpsimd.tensor_tensor(DB[:, p % NDB, :], REP[:, slot, NR + r, :], BC[:, d, k, :],
                                            ALU.mult).then_inc(dbu_ready, 1)
                    if front:
                        for _ in at("pool_rstd", p):
                            rstd_front(f)
                        for q in at("pool_du", p):
                            front_du(q, f, fp)
                    if back:
                        for _ in at("pool_a", p):
                            rstd_back("a", b)
                        for i in at("pool_ln", p):
                            (times_lnw, plus_lnb)[i](b)
                        for _ in at("pool_b", p):
                            rstd_back("b", b)
                        for _ in at("pool_res_b", p):
                            residual_b(b)
                        for _ in at("pool_c", p):
                            rstd_back("c", b)
                        for _ in at("pool_d", p):
                            rstd_back("d", b)
                if back:
                    residual_d(b)

            nc.gpsimd.memset(ident[:, :], 0.0).then_inc(const_ok, 1)
            nc.gpsimd.memset(mhalf[:, :], -0.5)
            nc.gpsimd.memset(zero2[:, :], 0.0)
            nc.gpsimd.memset(root[:, :], -(3.0 ** 0.5) / 4)
            nc.gpsimd.memset(ones[:, :], 1.0)
            nc.gpsimd.memset(XNT[:, :, :, :], 0.0)
            pool.wait_ge(const_ok, 1)
            nc.gpsimd.affine_select(out=ident[:, :], in_=ident[:, :], compare_op=ALU.not_equal, fill=1.0,
                                    base=0, pattern=[[-1, 128]], channel_multiplier=1).then_inc(const_ok, 1)
            pool.wait_ge(const_ok, 2)
            rstd_front(0)
            for q in range(NQ):
                front_du(q, 0, 0)
            end_first(pool, "pool")
            pool.wait_ge(w_back, 16 * N_BACK)
            iteration(0, 0, True, False)
            with pool.Fori(0, G // 2 - 1) as i:
                iteration(2 * i + 1, 1, True, True)
                iteration(2 * i + 2, 0, True, True)
            iteration(G - 1, 1, False, True)
            b = G - 1
            rstd_back("a", b)
            times_lnw(b)
            plus_lnb(b)
            rstd_back("b", b)
            residual_b(b)
            rstd_back("c", b)
            rstd_back("d", b)
            residual_d(b)

        @block.scalar
        def _(act):
            act_fn = nc.scalar.activation

            def front_xT(f, par):
                after(act, "pe_front", "xT", f)
                after(act, "pe_back", "combine", f - 2)
                act_fn(XNT[:, par, :, PAD:PAD + L], GF[:, :].rearrange("p (s l) -> p s l", s=SPG),
                       ACT.Copy).then_inc(front_sem("act", f), 1)

            def front_conv(q, f, par):
                after(act, "pe_front", f"conv{q}", f)
                act_fn(U[:, par, q, :], front_psum(f"conv{q}")[:, :], ACT.Identity, bias=cb[:, q:q + 1]).then_inc(front_sem("act", f), 1)

            def front_z(q, f, par):
                after(act, "pe_front", f"z{q}", f)
                act_fn(SZ[:, par, q, :], GF[:, :], ACT.Copy).then_inc(front_sem("act", f), 1)

            def first_silu_u(q):
                after(act, "pe_front", f"conv{q}", 0)
                act_fn(U[:, 0, q, :], front_psum(f"conv{q}", 0)[:, :], ACT.Silu, bias=cb[:, q:q + 1]).then_inc(act_first, 1)

            def first_silu_z(q):
                after(act, "pe_front", f"z{q}", 0)
                act_fn(SZ[:, 0, q, :], front_psum(f"z{q}", 0)[:, :], ACT.Silu).then_inc(act_first, 1)

            def silu_u(q, f, par):
                after(act, "act_front", f"conv{q}", f)
                act_fn(U[:, par, q, :], U[:, par, q, :], ACT.Silu).then_inc(front_sem("act", f), 1)

            def silu_z(q, f, par):
                after(act, "act_front", f"z{q}", f)
                act_fn(SZ[:, par, q, :], SZ[:, par, q, :], ACT.Silu).then_inc(front_sem("act", f), 1)

            def silu_a(m, b):
                after(act, "act_back", f"a{m}", b)
                act_fn(FA[:, m, :], FA[:, m, :], ACT.Silu).then_inc(act_back, 1)

            def exp_and_ln_tables():
                nc.scalar.add_instruction(mybir.InstLoadActFuncSet(
                    act_func_set_id=6, name=nc.get_next_instruction_name(), engine=nc.scalar.engine, ins=[], outs=[]))

            def front_xd(d, f):
                after(act, "pe_front", f"xd{d}", f)
                if not (isinstance(f, int) and f < 1):
                    wait(act, bc_out, f * 32)
                act_fn(x_dbl(f)[:, d, :], front_psum(f"xd{d}")[0:RANK + 2 * NS, :], ACT.Copy).then_inc(front_sem("act", f), 1)

            def front_dt(q, f):
                after(act, "pe_front", f"dt{q}", f)
                if not (isinstance(f, int) and f < 1):
                    wait(act, dd_out[q], f * 32)
                act_fn(SPA[:, q, :], front_psum(f"dt{q}")[:, :], ACT.Identity, bias=db[:, q:q + 1]).then_inc(front_sem("act", f), 1)

            def front_soft(n, q, f):
                if n == "abs":
                    after(act, "act_front", f"dt{q}", f)
                    act_fn(SPB[:, q, :], SPA[:, q, :], ACT.Abs).then_inc(front_sem("act", f), 1)
                if n == "exp":
                    after(act, "act_front", f"abs{q}", f)
                    act_fn(SPB[:, q, :], SPB[:, q, :], ACT.Exp, scale=-1.0).then_inc(front_sem("act", f), 1)
                if n == "square":
                    after(act, "act_front", f"exp{q}", f)
                    if not (isinstance(f, int) and f == 0 and q in HALVES[0]):
                        act.wait_ge(bc_out, 32 * (f + 1))
                    act_fn(FG[:, q, :], SPB[:, q, :], ACT.Square, scale=3.0 ** -0.5,
                           bias=root[:, 0:1]).then_inc(front_sem("act", f), 1)

            def front_ln(q, f):
                after(act, "dve_front", f"large{q}", f)
                act_fn(SPB[:, q, :], SPB[:, q, :], ACT.Ln, bias=1.0).then_inc(front_sem("act", f), 1)

            def back_xT(b):
                after(act, "pe_back", "xT", b)
                act_fn(X2T[:, :], GB[1][:, :], ACT.Copy).then_inc(act_back, 1)

            def back_a(m, b):
                after(act, "pe_back", f"a{m}", b)
                act_fn(FA[:, m, :], GB[m % 2][:, :], ACT.Copy, scale=s1c[:, m:m + 1]).then_inc(act_back, 1)

            def back_h(n, m, b):
                dst, col = ((FG, h1c), (FA, h2c))[n - 1]
                if n == 1 and m == 0 and not (isinstance(b, int) and b > G - 3):
                    after(act, "dve_front", f"delta{NQ - 1}", b + 2)
                after(act, "pe_back", f"h{n}_{m}", b)
                act_fn(dst[:, m, :], GB[m % 2][:, :], ACT.Copy, scale=col[:, m:m + 1]).then_inc(act_back, 1)

            def gelu(n, m, b):
                buf = (FG, FA)[n - 1]
                after(act, "act_back", f"h{n}_{m}", b)
                act_fn(buf[:, m, :], buf[:, m, :], ACT.Gelu).then_inc(act_back, 1)

            def iteration(g, par, front, back):
                f, b, fp = g + 1, g - 1, 1 - par
                for p in range(UNITS):
                    d, dt, k, r = unit(p)
                    slot = (p // UQ) % 2
                    first = 0 if d == 0 else L - 1
                    lo, hi = (1, L) if d == 0 else (0, L - 1)
                    wait(act, scan_done, g * UNITS + p - 1)
                    if p % (2 * UQ) < 2:
                        act_fn(dA[p % 2][:, :, first], zero2[:, :], ACT.Copy).then_inc(zero_set, 1)
                    if p % UQ == 0:
                        act.wait_ge(rep_in[slot], 64 * (2 * g + p // UQ // 2 + 1))
                    act_fn(dA[p % 2][:, :, lo:hi],
                           REP[:, slot, r, :].rearrange("p (s l) -> p s l", s=SPG)[:, :, lo:hi],
                           ACT.Exp, scale=AR[:, 8 * d + NR * dt + r, k:k + 1]).then_inc(dA_ready, 1)
                    if front:
                        for _ in at("act_xT", p):
                            front_xT(f, fp)
                        for q in at("act_conv", p):
                            front_conv(q, f, fp)
                        for q in at("act_xd", p):
                            front_xd(q, f)
                        for q in at("act_dt", p):
                            front_dt(q, f)
                        for s_ in at("act_soft", p):
                            for n, q in SOFT:
                                if ("abs", "exp", "square").index(n) + q == s_:
                                    front_soft(n, q, f)
                        for q in at("act_ln", p):
                            front_ln(q, f)
                        for q in at("act_z", p):
                            front_z(q, f, fp)
                    if back:
                        for _ in at("act_bxT", p):
                            back_xT(b)
                        for m in at("act_a", p):
                            back_a(m, b)
                        for m in at("act_h1", p):
                            back_h(1, m, b)
                        for m in at("act_h2", p):
                            back_h(2, m, b)
                    if front:
                        for q in at("act_silu_u", p):
                            silu_u(q, f, fp)
                        for q in at("act_silu_z", p):
                            silu_z(q, f, fp)
                    if back:
                        for m in at("act_silu_a", p):
                            silu_a(m, b)
                        for n in (1, 2):
                            for m in at(f"act_gelu{n}", p):
                                gelu(n, m, b)
                    if any(p in AT[n] for n in (["act_silu_u", "act_silu_z"] if front else [])
                           + (["act_silu_a", "act_gelu1", "act_gelu2"] if back else [])):
                        exp_and_ln_tables()

            exp_and_ln_tables()
            act.wait_ge(const_ok, 2)
            act.wait_ge(w_conv, 16 * N_CONV)
            front_xT(0, 0)
            for d, half in enumerate(HALVES):
                for q in half:
                    first_silu_u(q)
                if d == 1:
                    for q in range(NQ):
                        first_silu_z(q)
                exp_and_ln_tables()
                if d == 0:
                    act.wait_ge(w_front, 16 * N_FRONT)
                    act_fn(AR[:, :, :], AR[:, :, :], ACT.Exp).then_inc(a_exp, 1)
                front_xd(d, 0)
                for q in half:
                    front_dt(q, 0)
                for n in ("abs", "exp", "square"):
                    for q in half:
                        front_soft(n, q, 0)
                for q in half:
                    front_ln(q, 0)
            end_first(act, "act")
            act.wait_ge(we_pe, 1)
            act_fn(WE[:, :, :], GB[0][:, :].rearrange("p (q c) -> p q c", c=C), ACT.Copy).then_inc(we_act, 1)
            act.wait_ge(dprep, DVE_SETUP.index("a_rep") + 1)
            iteration(0, 0, True, False)
            with act.Fori(0, G // 2 - 1) as i:
                iteration(2 * i + 1, 1, True, True)
                iteration(2 * i + 2, 0, True, True)
            iteration(G - 1, 1, False, True)
            after(act, "pe_tail", "xT", 0)
            act_fn(X2T[:, :], SET2[2], ACT.Copy).then_inc(act_tail, 1)
            for m in range(HT):
                after(act, "pe_tail", f"a{m}", 0)
                act_fn(FA[:, m, :], SET1[m], ACT.Silu, scale=s1c[:, m:m + 1]).then_inc(act_tail, 1)
            for n, dst, col, banks in ((1, FG, h1c, SET1), (2, FA, h2c, SET2)):
                for m in range(HT):
                    after(act, "pe_tail", f"h{n}_{m}", 0)
                    act_fn(dst[:, m, :], banks[m], ACT.Gelu, scale=col[:, m:m + 1]).then_inc(act_tail, 1)

        @block.vector
        def _(dve):
            def done(table, step, g):
                after(dve, table, step, g)

            def stats(src, st, s_):
                for t in range(NT):
                    i_ = nc.vector.bn_stats(st[:, t, :], src[:, t, :])
                i_.then_inc(s_, 1)

            def aggregate(n, st, mv, rs, stage, s_, g):
                for t in range(NT):
                    i_ = nc.vector.bn_aggr(mv[:, t, :], st[:, t, :])
                i_.then_inc(s_, 1)
                done(stage, "aggr" + n, g)
                nc.vector.tensor_scalar(rs[:, 0, :], mv[:, :, 1], EPS, None, ALU.add).then_inc(s_, 1)

            def normalise(dst, src, mv, rs, s_):
                for t in range(NT):
                    i_ = nc.vector.tensor_scalar(dst[:, t, :], src[:, t, :], mv[:, t, 0:1], rs[:, 1, t:t + 1],
                                                 ALU.subtract, ALU.mult)
                i_.then_inc(s_, 1)

            def front_moments(f):
                dve.wait_ge(x_in, 16 * (f + 1))
                stats(XT, STF, front_sem("dve", f))

            def front_aggregate(f):
                aggregate("", STF, MVF, RSF, "dve_front", front_sem("dve", f), f)

            def front_norm(f):
                done("pool_front", "rstd", f)
                normalise(XT, XT, MVF, RSF, front_sem("dve", f))

            def front_series(q, f):
                done("act_front", f"square{q}", f)
                nc.vector.scalar_tensor_tensor(FG[:, q, :], FG[:, q, :], 13.0 / 16, SPB[:, q, :],
                                               ALU.add, ALU.mult).then_inc(front_sem("dve", f), 1)
                nc.vector.tensor_scalar(big[:, q, :], SPB[:, q, :], SMALL, None, ALU.is_ge).then_inc(front_sem("dve", f), 1)

            def front_select_wait(q, f):
                done("dve_front", f"large{q}", f)
                done("act_front", f"ln{q}", f)

            def front_select(q, f):
                nc.vector.copy_predicated(FG[:, q, :], big[:, q, :], SPB[:, q, :]).then_inc(front_sem("dve", f), 1)

            def front_delta(q, f):
                done("dve_front", f"select{q}", f)
                nc.vector.scalar_tensor_tensor(SPB[:, q, :], SPA[:, q, :], 0.0, FG[:, q, :],
                                               ALU.max, ALU.add).then_inc(front_sem("dve", f), 1)

            def tokens(bank):
                return bank.rearrange("p (t c) -> p t c", c=C)

            bank0, tail_in, tail_out = tokens(GB[0][:, :]), tokens(GF[:, :]), tokens(SET1[0])

            def back_moments(n, b, tail=False):
                if n in "ad":
                    step = {"a": "combine", "d": "w3"}[n]
                    done("pe_tail", step, 0) if tail else done("pe_back", step, b)
                if n == "b":
                    done("pool_back", "lnb", b)
                if n == "c":
                    done("pool_back", "res_b", b)
                src = {"a": tail_in if tail else bank0, "b": TA, "c": X1, "d": tail_out if tail else bank0}[n]
                stats(src, STB, dve_back)

            def back_norm(n, b, tail=False):
                done("pool_back", "rstd_" + n, b)
                src = {"a": tail_in if tail else bank0, "b": TA, "c": X1, "d": tail_out if tail else bank0}[n]
                normalise(TA, src, MVB, RSB, dve_back)

            def back_b(m, b, tail=False):
                if tail:
                    done("pe_tail", f"b{m}", 0)
                    done("act_tail", f"a{m}", 0)
                else:
                    done("pe_back", f"b{m}", b)
                    done("act_back", f"silu{m}", b)
                nc.vector.scalar_tensor_tensor(FA[:, m, :], SET2[m] if tail else GB[m % 2][:, :], s2c[:, m:m + 1],
                                               FA[:, m, :], ALU.mult, ALU.mult).then_inc(dve_back, 1)

            def back_aggregate(n, b):
                aggregate("_" + n, STB, MVB, RSB, "dve_back", dve_back, b)

            def gate(q, g, par):
                wait(dve, y_ready, NQ * g + q + 1)
                nc.vector.tensor_tensor(SZ[:, par, q, :], Y[:, :], SZ[:, par, q, :], ALU.mult).then_inc(gated, 1)

            def scan(p, g):
                d = unit(p)[0]
                wait(dve, dA_ready, g * UNITS + p + 1)
                wait(dve, dbu_ready, g * UNITS + p + 1)
                wait(dve, prod_ready, g * UNITS + p - 1)
                a_, b_, h_ = dA[p % 2][:, :, :].rearrange("p s l -> p (s l)"), DB[:, p % NDB, :], HP[p % 2][:, :]
                if d == 1:
                    a_, b_, h_ = a_[:, ::-1], b_[:, ::-1], h_[:, ::-1]
                nc.vector.tensor_tensor_scan(h_, a_, b_, 0.0, ALU.mult, ALU.add).then_inc(scan_done, 1)

            def product(p, g):
                d, dt, k, r = unit(p)
                if p % (2 * UQ) == 0:
                    dve.wait_ge(bc_in[d], 64 * (g + 1))
                if p % NR == 0:
                    wait(dve, sums_done, UNITS // NR * g + p // NR - 1)
                wait(dve, scan_done, g * UNITS + p + 1)
                nc.vector.tensor_tensor(PR[:, (p // NR) % 2, r, :], HP[p % 2][:, :], BC[:, d, NK + k, :],
                                        ALU.mult).then_inc(prod_ready, 1)

            def iteration(g, par, front, back):
                f, b, fp = g + 1, g - 1, 1 - par
                for p in range(UNITS):
                    if p % 2 == 0:
                        scan(p, g)
                        scan(p + 1, g)
                    if front:
                        for _ in at("dve_stats", p - 1):
                            done("dve_front", "stats", f)
                        for q in at("dve_select", p):
                            front_select_wait(q, f)
                    if back:
                        for n in "abcd":
                            for _ in at("dve_" + n, p - 1):
                                done("dve_back", "stats_" + n, b)
                    product(p, g)
                    for q in at("dve_gate", p):
                        gate(q, g, par)
                    if back:
                        for _ in at("dve_last_gate", p):
                            gate(NQ - 1, b, fp)
                        for n in "abcd":
                            for _ in at("dve_" + n, p - 1):
                                back_aggregate(n, b)
                            for _ in at("dve_" + n, p):
                                back_moments(n, b)
                        for n in "abc":
                            for _ in at("dve_norm_" + n, p):
                                back_norm(n, b)
                        for m in at("dve_mul", p):
                            back_b(m, b)
                    if front:
                        for _ in at("dve_stats", p - 1):
                            front_aggregate(f)
                        for _ in at("dve_stats", p):
                            front_moments(f)
                        for _ in at("dve_norm", p):
                            front_norm(f)
                        for q in at("dve_series", p):
                            front_series(q, f)
                        for q in at("dve_select", p):
                            front_select(q, f)
                            front_delta(q, f)
                if back:
                    back_norm("d", b)

            def tap(q):
                o = tapT[:, q // DT, :, 128 * (q % DT):128 * (q % DT + 1)]
                i_ = n_in[:, q // DT, 128 * (q % DT):128 * (q % DT + 1)].rearrange("p (a c) -> p a c", a=1)
                nc.vector.tensor_tensor(o, o, i_.to_broadcast([128, TAPS, 128]), ALU.mult).then_inc(dprep, 1)

            front_moments(0)
            done("dve_front", "stats", 0)
            front_aggregate(0)
            dve.wait_ge(w_conv, 16 * N_CONV)
            tap(0)
            front_norm(0)
            for q in range(1, NQ):
                tap(q)
            dve.wait_ge(const_ok, 2)
            nc.vector.tensor_reduce(fold[:, :], ident[:, :].rearrange("p (j d) -> p d j", d=DW), op=ALU.add,
                                    axis=AX.X).then_inc(dprep, 1)
            for q in range(NQ):
                i_ = nc.vector.tensor_scalar(DD[:, q, :], ident[:, :], dp[:, q:q + 1], None, ALU.mult)
            i_.then_inc(dprep, 1)
            dve.wait_ge(a_exp, 1)
            nc.vector.tensor_scalar(AR[:, :, :], AR[:, :, :], -1.0, None, ALU.mult).then_inc(dprep, 1)
            dve.wait_ge(w_comb, 16 * N_COMB)
            nc.vector.tensor_tensor(P12[:, :], PT[:, 0, :], PT[:, 1, :], ALU.add).then_inc(dprep, 1)
            for half in HALVES:
                for q in half:
                    front_series(q, 0)
                for q in half:
                    front_select_wait(q, 0)
                    front_select(q, 0)
                    front_delta(q, 0)
            end_first(dve, "dve")
            dve.wait_ge(w_back, 16 * N_BACK)
            nc.vector.tensor_tensor(w3T[:, :, :], w3T[:, :, :],
                                    w3row.rearrange("p (a c) -> p a c", a=1).to_broadcast([128, HT, C]),
                                    ALU.mult).then_inc(dprep, 1)
            iteration(0, 0, True, False)
            with dve.Fori(0, G // 2 - 1) as i:
                iteration(2 * i + 1, 1, True, True)
                iteration(2 * i + 2, 0, True, True)
            iteration(G - 1, 1, False, True)
            b = G - 1
            gate(NQ - 1, b, 1)
            for n in "abc":
                back_moments(n, b, tail=True)
                done("dve_back", "stats_" + n, b)
                back_aggregate(n, b)
                back_norm(n, b, tail=True)
            for m in range(HT):
                back_b(m, b, tail=True)
            back_moments("d", b, tail=True)
            done("dve_back", "stats_d", b)
            back_aggregate("d", b)
            back_norm("d", b, tail=True)

        @block.tensor
        def _(pe):
            mm = nc.tensor.matmul

            def done(table, step, g):
                after(pe, table, step, g)

            def front_bank(step, f):
                order = PE_FIRST if isinstance(f, int) and f == 0 else PE_FRONT
                before = [s_ for s_ in order[:order.index(step)] if front_psum(s_, f) is front_psum(step, f)]
                if before:
                    done("act_front", before[-1], f)
                elif step == "xT":
                    done("act_front", PE_FRONT[-1], f - 1)

            def front_xT(f):
                front_bank("xT", f)
                done("dve_front", "norm", f)
                for t in range(NT):
                    i_ = nc.tensor.transpose(GF[:, 128 * t:128 * (t + 1)], XT[:, t, :], ident[:, :])
                i_.then_inc(front_sem("pe", f), 1)

            def front_conv(q, f, par):
                d, t = q // DT, q % DT
                front_bank(f"conv{q}", f)
                for k in range(TAPS):
                    at = k if d == 0 else 2 * PAD - k
                    i_ = mm(front_psum(f"conv{q}")[:, :], tapT[:, d, k, 128 * t:128 * (t + 1)], XNT[:, par, :, at:at + L],
                            start=(k == 0), stop=(k == TAPS - 1))
                i_.then_inc(front_sem("pe", f), 1)

            def front_z(q, f, par):
                front_bank(f"z{q}", f)
                mm(front_psum(f"z{q}", f)[:, :], zT[:, q, :], XNT[:, par, :, PAD:PAD + L], start=True, stop=True).then_inc(front_sem("pe", f), 1)

            def front_xd(d, f, par, back=False):
                done("act_front", f"silu_u{DT * d + DT - 1}", f)
                if d == 1 and back:
                    done("dve_back", "norm_a", f - 2)
                front_bank(f"xd{d}", f)
                for t in range(DT):
                    i_ = mm(front_psum(f"xd{d}")[0:RANK + 2 * NS, :], xpT[:, d * DT + t, :], U[:, par, d * DT + t, :],
                            start=(t == 0), stop=(t == DT - 1))
                i_.then_inc(front_sem("pe", f), 1)

            def front_dt(q, f):
                front_bank(f"dt{q}", f)
                done("act_front", f"xd{q // DT}", f)
                mm(front_psum(f"dt{q}")[:, :], dtT[:, q, :], x_dbl(f)[0:RANK, q // DT, :], start=True, stop=True).then_inc(front_sem("pe", f), 1)

            def combine(b, par):
                wait(pe, gated, NQ * (b + 1))
                for t in range(NT):
                    o = GB[0][:, C * t:C * (t + 1)]
                    tok = slice(128 * t, 128 * (t + 1))
                    for q in range(NQ):
                        mm(o, SZ[:, par, q, tok], WE[:, q, :], start=(q == 0), stop=False)
                    s_, h_ = t * 128 // L, t * 128 % L
                    mm(o, XNT[:, par, s_, PAD + h_:PAD + h_ + 128], P12[:, :], start=False, stop=False)
                    i_ = mm(o, ones[:, :], pbrow[:, :], start=False, stop=True)
                i_.then_inc(pe_back, 1)

            def back_xT(b, front=False):
                done("dve_back", "norm_c", b)
                if front:
                    done("act_front", "conv3", b + 2)
                for t in range(NT):
                    i_ = nc.tensor.transpose(GB[1][:, 128 * t:128 * (t + 1)], TA[:, t, :], ident[:, :])
                i_.then_inc(pe_back, 1)

            def back_up(n, m, b, front=False):
                w_ = {"a": w1T, "b": w2T}[n]
                if n == "a":
                    done("act_back", "xT", b)
                    done("dve_back", "norm_a", b) if m == 0 else None
                    done("act_back", f"a{m - 2}", b) if m >= 2 else None
                    if m == 0 and front:
                        done("act_front", "dt3", b + 2)
                else:
                    done("act_back", f"a{m + 2}", b) if m < 2 else done("dve_back", f"b{m - 2}", b)
                mm(GB[m % 2][:, :], w_[:, 128 * m:128 * (m + 1)], X2T[:, :], start=True, stop=True).then_inc(pe_back, 1)

            def back_h(n, m, b):
                w_, src = ((h1T, FA), (h2T, FG))[n - 1]
                if n == 1:
                    done("dve_back", f"b{HT - 1}", b)
                elif m == 0:
                    done("act_back", f"h1_{HT - 1}", b)
                if m >= 2:
                    done("act_back", f"h{n}_{m - 2}", b)
                for k in range(HT):
                    if n == 2 and m == 0:
                        done("act_back", f"gelu1_{k}", b)
                    i_ = mm(GB[m % 2][:, :], w_[:, k, 128 * m:128 * (m + 1)], src[:, k, :],
                            start=(k == 0), stop=(k == HT - 1))
                i_.then_inc(pe_back, 1)

            def back_w3(b):
                done("act_back", f"gelu2_{HT - 1}", b)
                for t in range(NT):
                    for k in range(HT):
                        i_ = mm(GB[0][:, C * t:C * (t + 1)], FA[:, k, 128 * t:128 * (t + 1)], w3T[:, k, :],
                                start=(k == 0), stop=(k == HT - 1))
                i_.then_inc(pe_back, 1)

            def sums(s_, g, par):
                q = s_ * NR // UQ
                last = s_ % NK == NK - 1
                if s_ % NK == 0:
                    wait(pe, gated, NQ * g + q)
                    mm(Y[:, :], DD[:, q, :], U[:, par, q, :], start=True, stop=False)
                wait(pe, prod_ready, g * UNITS + NR * (s_ + 1))
                for r in range(NR):
                    i_ = mm(Y[DW * r:DW * (r + 1), :], fold[:, :], PR[:, s_ % 2, r, :], start=False, stop=last)
                i_.then_inc(sums_done, 1)
                if last:
                    pe.wait_ge(sums_done, UNITS // NR * g + s_ + 1)
                    pe.sem_inc(y_ready, 1)

            def iteration(g, par, front, back):
                f, b, fp = g + 1, g - 1, 1 - par
                late = AT["pe_sums"][0]
                for p in range(UNITS):
                    if p % NR == late and p > NR:
                        sums(p // NR - 1, g, par)
                    if back:
                        for _ in at("pe_combine", p):
                            combine(b, fp)
                        for _ in at("pe_bxT", p):
                            back_xT(b, front)
                        for m in at("pe_a", p):
                            back_up("a", m, b, front)
                        for m in at("pe_b", p):
                            back_up("b", m, b)
                        for n in (1, 2):
                            for m in at(f"pe_h{n}", p):
                                back_h(n, m, b)
                        for _ in at("pe_w3", p):
                            back_w3(b)
                    if front:
                        for _ in at("pe_xT", p):
                            front_xT(f)
                        for q in at("pe_conv", p):
                            front_conv(q, f, fp)
                        for d in at("pe_xd", p):
                            front_xd(d, f, fp, back)
                        for q in at("pe_dt", p):
                            front_dt(q, f)
                        for q in at("pe_z", p):
                            front_z(q, f, fp)
                    if g is last_group and p == UNITS - 3:
                        tail_combine(False)
                sums(UNITS // NR - 1, g, par)

            last_group = G - 1

            def tail_combine(end):
                if not end:
                    wait(pe, gated, NQ * G - 1)
                    done("act_front", ACT_FRONT[-1], G - 1)
                else:
                    wait(pe, gated, NQ * G)
                for t in range(NT):
                    o = GF[:, C * t:C * (t + 1)]
                    tok = slice(128 * t, 128 * (t + 1))
                    if end:
                        i_ = mm(o, SZ[:, 1, NQ - 1, tok], WE[:, NQ - 1, :], start=False, stop=(t == NT - 1))
                    else:
                        for q in range(NQ - 1):
                            mm(o, SZ[:, 1, q, tok], WE[:, q, :], start=(t == 0 and q == 0), stop=False)
                        s_, h_ = t * 128 // L, t * 128 % L
                        mm(o, XNT[:, 1, s_, PAD + h_:PAD + h_ + 128], P12[:, :], start=False, stop=False)
                        mm(o, ones[:, :], pbrow[:, :], start=False, stop=False)
                if end:
                    i_.then_inc(pe_tail, 1)

            pe.wait_ge(const_ok, 2)
            front_xT(0)
            for d, half in enumerate(HALVES):
                for q in half:
                    pe.wait_ge(dprep, DVE_SETUP.index(f"tap{q}") + 1)
                    front_conv(q, 0, 0)
                if d == 0:
                    pe.wait_ge(w_front, 16 * N_FRONT)
                else:
                    for q in range(NQ):
                        front_z(q, 0, 0)
                front_xd(d, 0, 0)
                for q in half:
                    front_dt(q, 0)
            end_first(pe, "pe")
            done("act_front", "dt3", 0)
            pe.wait_ge(w_comb, 16 * N_COMB)
            for q in range(NQ):
                i_ = mm(GB[0][:, C * q:C * (q + 1)], n_out[:, q, :], PT[:, q // DT, :], start=True, stop=True)
            i_.then_inc(we_pe, 1)
            pe.wait_ge(we_act, 1)
            pe.wait_ge(dprep, len(DVE_SETUP))
            pe.wait_ge(w_back, 16 * N_BACK)
            iteration(0, 0, True, False)
            with pe.Fori(0, G // 2 - 1) as i:
                iteration(2 * i + 1, 1, True, True)
                iteration(2 * i + 2, 0, True, True)
            iteration(G - 1, 1, False, True)
            b = G - 1
            tail_combine(True)
            done("dve_back", "norm_c", b)
            done("act_back", f"h2_{HT - 1}", b - 1)
            for t in range(NT):
                i_ = nc.tensor.transpose(SET2[2][:, 128 * t:128 * (t + 1)], TA[:, t, :], ident[:, :])
            i_.then_inc(pe_tail, 1)
            wait(pe, scan_done, UNITS * G)
            wait(pe, prod_ready, UNITS * G)
            done("act_tail", "xT", 0)
            for w_, banks in ((w1T, SET1), (w2T, SET2)):
                for m in range(HT):
                    mm(banks[m], w_[:, 128 * m:128 * (m + 1)], X2T[:, :], start=True, stop=True).then_inc(pe_tail, 1)
            for n, w_, src, banks in ((1, h1T, FA, SET1), (2, h2T, FG, SET2)):
                for k in range(HT):
                    done("dve_back", f"b{k}", b) if n == 1 else done("act_tail", f"h1_{k}", 0)
                    for m in range(HT):
                        if n == 1 and k == 0:
                            done("act_tail", f"a{m}", 0)
                        i_ = mm(banks[m], w_[:, k, 128 * m:128 * (m + 1)], src[:, k, :],
                                start=(k == 0), stop=(k == HT - 1))
                        if k == HT - 1:
                            i_.then_inc(pe_tail, 1)
            for k in range(HT):
                done("act_tail", f"h2_{k}", 0)
                for t in range(NT):
                    i_ = mm(SET1[0][:, C * t:C * (t + 1)], FA[:, k, 128 * t:128 * (t + 1)], w3T[:, k, :],
                            start=(t == 0 and k == 0), stop=(t == NT - 1 and k == HT - 1))
            i_.then_inc(pe_tail, 1)


def kernel(L0_attn_x, L0_attn_proj_w, L0_attn_proj_b, L0_attn_ln_w, L0_attn_ln_b, **rest):
    import numpy as _np
    import concourse.bacc as _bacc
    from concourse import mybir as _mybir
    from concourse.bass_utils import run_bass_kernel_spmd as _run

    def both(name):
        return _np.stack([_np.asarray(rest[f"L0_attn_{d}_{name}"]) for d in ("fw", "bw")])

    def ffn(name):
        return _np.asarray(rest[f"L0_ffn_{name}"])

    def columns(v):
        return v.reshape(-1, 128).T

    def rows_on_partitions(w_t):
        return w_t.reshape(-1, 128, w_t.shape[-1]).transpose(1, 0, 2)

    laid = {
        "x": _np.asarray(L0_attn_x),
        "in_t": both("in_w").transpose(2, 0, 1),
        "taps": both("conv_w")[:, :, 0, :].transpose(0, 2, 1).reshape(1, -1),
        "xproj_t": rows_on_partitions(both("xproj_w").transpose(0, 2, 1).reshape(2 * DI, -1)),
        "dt_t": both("dt_w").transpose(2, 0, 1).reshape(RANK, NQ, 128),
        "a_log": both("Alog").reshape(2, DI // DW, DW, NK, NJ).transpose(4, 2, 0, 1, 3).reshape(128, -1, NK),
        "columns": _np.concatenate([columns(v) for v in (both("conv_b"), both("dt_b"), both("Dp"), ffn("w1_s"),
                                                         ffn("w2_s"), ffn("h1_s"), ffn("h2_s"))], axis=1),
        "out_w": both("out_w").transpose(1, 0, 2).reshape(128, NQ, 128),
        "proj_t": _np.asarray(L0_attn_proj_w).T.reshape(2, C, C).transpose(1, 0, 2),
        "proj_b": _np.asarray(L0_attn_proj_b).reshape(1, C),
        "ln_w": _np.asarray(L0_attn_ln_w).reshape(1, C),
        "ln_b": _np.asarray(L0_attn_ln_b).reshape(1, C),
        "w1_t": ffn("w1_w").T, "w2_t": ffn("w2_w").T,
        "h1_t": rows_on_partitions(ffn("h1_w").T), "h2_t": rows_on_partitions(ffn("h2_w").T),
        "w3_t": rows_on_partitions(ffn("w3_w").T), "w3_s": ffn("w3_s").reshape(1, C),
    }
    nc = _bacc.Bacc("TRN2", target_bir_lowering=False, num_devices=1)
    arrays, args = {}, {}
    for name, a in laid.items():
        a = _np.ascontiguousarray(a)
        arrays[f"in_{name}_dram"] = a
        args[name] = nc.dram_tensor(f"in_{name}_dram", a.shape, _mybir.dt.from_np(a.dtype), kind="ExternalInput").ap()
    out = nc.dram_tensor("out_0_dram", (SEQS, L, C), _mybir.dt.float32, kind="ExternalOutput").ap()
    build(nc, args.pop("x"), args, out)
    r = _run(nc, [arrays], core_ids=[0])
    return r.results[0]["out_0_dram"]
```
